# Optimizing a Trainium2 kernel written in Bass

```python
import numpy as np
import jax
import jax.numpy as jnp

def _softmax(x, axis=-1):
    return jax.nn.softmax(x, axis=axis)

def _gelu(x):
    return jax.nn.gelu(x, approximate=True)

def _silu(x):
    return jax.nn.silu(x)

def _sigmoid(x):
    return jax.nn.sigmoid(x)

def _layernorm(x, axis=-1, eps=1e-05):
    m = jnp.mean(x, axis=axis, keepdims=True)
    v = jnp.var(x, axis=axis, keepdims=True)
    return (x - m) / jnp.sqrt(v + eps)

def _scatter_add(tgt, idx, src, axis=0):
    return tgt.at[idx].add(src)

def _segment_sum(src, seg, n):
    return jax.ops.segment_sum(src, seg, n)
kernel_name = 'mk_adaln_attn_ffn_d1_seqx_r4_f3e687'

def setup_inputs(seed: int=0):
    np.random.seed(seed)
    _w = jnp.asarray

    def _rec_inputs():
        import jax
        import jax.numpy as jnp
        _rk = jax.random.key(seed)
        x = -0.000125 + 0.9999 * jax.random.normal(jax.random.fold_in(_rk, 1), (4, 512, 512), jnp.float32)
        _lenS = 512 - jax.random.randint(jax.random.fold_in(_rk, 7), (4,), 0, max(1, 512 // 4) + 1, jnp.int32)
        _lenS2 = 512 - jax.random.randint(jax.random.fold_in(_rk, 8), (4,), 0, max(1, 512 // 4) + 1, jnp.int32)
        fside_BxSxS_0 = -1.52775e-05 + 0.999936 * jax.random.normal(jax.random.fold_in(_rk, 11), (4, 512, 512), jnp.float32)
        cond_512 = -5.03954e-05 + 1.00559 * jax.random.normal(jax.random.fold_in(_rk, 12), (4, 128), jnp.float32)
        return (x, fside_BxSxS_0, cond_512)
    x, fside_BxSxS_0, cond_512 = _rec_inputs()

    def _L0_cond_setup():
        import jax, jax.numpy as jnp
        from jax import lax
        import numpy as np
        B, T, C, TD = (8, 512, 512, 128)

        def _bi_wkv(r, k, v, w, u, time_emb):
            tf = jax.nn.sigmoid(jnp.sum(time_emb, axis=-1))[:, None, None]
            decay = jnp.exp(-jnp.exp(w.astype(jnp.float32)))[None, :] * (0.5 + 0.5 * tf[:, :, 0])
            kf = k.astype(jnp.float32)
            vf = v.astype(jnp.float32)
            ek = jnp.exp(jnp.minimum(kf, 30.0))
            ekv = ek * vf

            def step(carry, x):
                a, b = carry
                ekv_t, ek_t = x
                a = a * decay + ekv_t
                b = b * decay + ek_t
                return ((a, b), (a, b))
            ekv_t = jnp.swapaxes(ekv, 0, 1)
            ek_t = jnp.swapaxes(ek, 0, 1)
            init = (jnp.zeros_like(decay), jnp.zeros_like(decay))
            _, (nf, df) = lax.scan(step, init, (ekv_t, ek_t))
            _, (nb, db) = lax.scan(step, init, (ekv_t, ek_t), reverse=True)
            nf = jnp.swapaxes(nf, 0, 1)
            df = jnp.swapaxes(df, 0, 1)
            nb = jnp.swapaxes(nb, 0, 1)
            db = jnp.swapaxes(db, 0, 1)
            euk = jnp.exp(jnp.minimum(u.astype(jnp.float32)[None, None, :] + kf, 30.0))
            num = nf + nb - ekv + euk * vf
            den = df + db - ek + euk
            base = jax.nn.sigmoid(r.astype(jnp.float32)) * (num / jnp.maximum(den, 1e-08))
            out = base * (0.8 + 0.2 * tf)
            return out.astype(r.dtype)
        key = jax.random.key(seed)
        ks = jax.random.split(key, 6)
        return {'r': jax.random.normal(ks[0], (B, T, C), dtype=jnp.float32), 'k': jax.random.normal(ks[1], (B, T, C), dtype=jnp.float32), 'v': jax.random.normal(ks[2], (B, T, C), dtype=jnp.float32), 'w': jax.random.normal(ks[3], (C,), dtype=jnp.float32), 'u': jax.random.normal(ks[4], (C,), dtype=jnp.float32), 'time_emb': jax.random.normal(ks[5], (B, TD), dtype=jnp.float32)}
    _L0_cond_all = _L0_cond_setup()
    _L0_cond_in = {k: v for k, v in _L0_cond_all.items() if k in ('w', 'u')}
    del _L0_cond_all

    def _L0_attn_setup():
        import jax, jax.numpy as jnp
        import numpy as np
        B, S, D = (2, 1024, 512)
        H, DK, DV = (16, 128, 128)
        SEG = 128
        UPDATE = 'delta'
        CAUSAL = True
        key = jax.random.key(seed)
        ks = jax.random.split(key, 6)
        s = 0.02
        return {'x': jax.random.normal(ks[0], (B, S, D), jnp.float32), 'Wq': jax.random.normal(ks[1], (D, H * DK), jnp.float32) * s, 'Wk': jax.random.normal(ks[2], (D, H * DK), jnp.float32) * s, 'Wv': jax.random.normal(ks[3], (D, H * DV), jnp.float32) * s, 'Wo': jax.random.normal(ks[4], (H * DV, D), jnp.float32) * s, 'betas': jax.random.normal(ks[5], (1, H, 1, DV), jnp.float32)}
    _L0_attn_all = _L0_attn_setup()
    _L0_attn_in = {k: v for k, v in _L0_attn_all.items() if k in ('Wq', 'Wk', 'Wv', 'Wo', 'betas')}
    del _L0_attn_all

    def _L0_cond2_setup():
        import jax, jax.numpy as jnp
        from jax import lax
        import numpy as np
        B, T, C, TD = (8, 512, 512, 128)

        def _bi_wkv(r, k, v, w, u, time_emb):
            tf = jax.nn.sigmoid(jnp.sum(time_emb, axis=-1))[:, None, None]
            decay = jnp.exp(-jnp.exp(w.astype(jnp.float32)))[None, :] * (0.5 + 0.5 * tf[:, :, 0])
            kf = k.astype(jnp.float32)
            vf = v.astype(jnp.float32)
            ek = jnp.exp(jnp.minimum(kf, 30.0))
            ekv = ek * vf

            def step(carry, x):
                a, b = carry
                ekv_t, ek_t = x
                a = a * decay + ekv_t
                b = b * decay + ek_t
                return ((a, b), (a, b))
            ekv_t = jnp.swapaxes(ekv, 0, 1)
            ek_t = jnp.swapaxes(ek, 0, 1)
            init = (jnp.zeros_like(decay), jnp.zeros_like(decay))
            _, (nf, df) = lax.scan(step, init, (ekv_t, ek_t))
            _, (nb, db) = lax.scan(step, init, (ekv_t, ek_t), reverse=True)
            nf = jnp.swapaxes(nf, 0, 1)
            df = jnp.swapaxes(df, 0, 1)
            nb = jnp.swapaxes(nb, 0, 1)
            db = jnp.swapaxes(db, 0, 1)
            euk = jnp.exp(jnp.minimum(u.astype(jnp.float32)[None, None, :] + kf, 30.0))
            num = nf + nb - ekv + euk * vf
            den = df + db - ek + euk
            base = jax.nn.sigmoid(r.astype(jnp.float32)) * (num / jnp.maximum(den, 1e-08))
            out = base * (0.8 + 0.2 * tf)
            return out.astype(r.dtype)
        key = jax.random.key(seed)
        ks = jax.random.split(key, 6)
        return {'r': jax.random.normal(ks[0], (B, T, C), dtype=jnp.float32), 'k': jax.random.normal(ks[1], (B, T, C), dtype=jnp.float32), 'v': jax.random.normal(ks[2], (B, T, C), dtype=jnp.float32), 'w': jax.random.normal(ks[3], (C,), dtype=jnp.float32), 'u': jax.random.normal(ks[4], (C,), dtype=jnp.float32), 'time_emb': jax.random.normal(ks[5], (B, TD), dtype=jnp.float32)}
    _L0_cond2_all = _L0_cond2_setup()
    _L0_cond2_in = {k: v for k, v in _L0_cond2_all.items() if k in ('w', 'u')}
    del _L0_cond2_all

    def _L0_ffn_setup():
        import jax, jax.numpy as jnp
        import numpy as np
        B, S, D, H = (4, 512, 512, 2048)

        def fwht(x):
            orig_shape = x.shape
            n = orig_shape[-1]
            x = x.reshape(-1, n)
            h = 1
            while h < n:
                xb = x.reshape(-1, n // (2 * h), 2, h)
                a = xb[:, :, 0, :]
                b = xb[:, :, 1, :]
                x = jnp.stack([a + b, a - b], axis=2).reshape(-1, n)
                h *= 2
            scale = jnp.asarray(1.0 / np.sqrt(n), dtype=x.dtype)
            return (x * scale).reshape(orig_shape)
        key = jax.random.key(seed)
        kx, k1, k2, k3 = jax.random.split(key, 4)
        x = jax.random.normal(kx, (B, S, D), dtype=jnp.float32)
        W1 = jax.random.normal(k1, (H, D), dtype=jnp.float32) * (1.0 / np.sqrt(D))
        W2 = jax.random.normal(k2, (D, H), dtype=jnp.float32) * (1.0 / np.sqrt(H))
        W3 = jax.random.normal(k3, (H, D), dtype=jnp.float32) * (1.0 / np.sqrt(D))
        return {'x': x, 'W1': W1, 'W2': W2, 'W3': W3}
    _L0_ffn_all = _L0_ffn_setup()
    _L0_ffn_in = {k: v for k, v in _L0_ffn_all.items() if k in ('W1', 'W2', 'W3')}
    del _L0_ffn_all
    return {'x': x, 'fside_BxSxS_0': fside_BxSxS_0, 'cond_512': cond_512, 'L0_cond_w': _L0_cond_in['w'], 'L0_cond_u': _L0_cond_in['u'], 'L0_attn_Wq': _L0_attn_in['Wq'], 'L0_attn_Wk': _L0_attn_in['Wk'], 'L0_attn_Wv': _L0_attn_in['Wv'], 'L0_attn_Wo': _L0_attn_in['Wo'], 'L0_attn_betas': _L0_attn_in['betas'], 'L0_cond2_w': _L0_cond2_in['w'], 'L0_cond2_u': _L0_cond2_in['u'], 'L0_ffn_W1': _L0_ffn_in['W1'], 'L0_ffn_W2': _L0_ffn_in['W2'], 'L0_ffn_W3': _L0_ffn_in['W3']}

def reference(x, fside_BxSxS_0, cond_512, L0_cond_w, L0_cond_u, L0_attn_Wq, L0_attn_Wk, L0_attn_Wv, L0_attn_Wo, L0_attn_betas, L0_cond2_w, L0_cond2_u, L0_ffn_W1, L0_ffn_W2, L0_ffn_W3):
    import jax
    import jax.numpy as jnp

    def _L0_cond_ref(r, k, v, w, u, time_emb):
        import jax, jax.numpy as jnp
        from jax import lax
        import numpy as np
        B, T, C, TD = (8, 512, 512, 128)

        def _bi_wkv(r, k, v, w, u, time_emb):
            tf = jax.nn.sigmoid(jnp.sum(time_emb, axis=-1))[:, None, None]
            decay = jnp.exp(-jnp.exp(w.astype(jnp.float32)))[None, :] * (0.5 + 0.5 * tf[:, :, 0])
            kf = k.astype(jnp.float32)
            vf = v.astype(jnp.float32)
            ek = jnp.exp(jnp.minimum(kf, 30.0))
            ekv = ek * vf

            def step(carry, x):
                a, b = carry
                ekv_t, ek_t = x
                a = a * decay + ekv_t
                b = b * decay + ek_t
                return ((a, b), (a, b))
            ekv_t = jnp.swapaxes(ekv, 0, 1)
            ek_t = jnp.swapaxes(ek, 0, 1)
            init = (jnp.zeros_like(decay), jnp.zeros_like(decay))
            _, (nf, df) = lax.scan(step, init, (ekv_t, ek_t))
            _, (nb, db) = lax.scan(step, init, (ekv_t, ek_t), reverse=True)
            nf = jnp.swapaxes(nf, 0, 1)
            df = jnp.swapaxes(df, 0, 1)
            nb = jnp.swapaxes(nb, 0, 1)
            db = jnp.swapaxes(db, 0, 1)
            euk = jnp.exp(jnp.minimum(u.astype(jnp.float32)[None, None, :] + kf, 30.0))
            num = nf + nb - ekv + euk * vf
            den = df + db - ek + euk
            base = jax.nn.sigmoid(r.astype(jnp.float32)) * (num / jnp.maximum(den, 1e-08))
            out = base * (0.8 + 0.2 * tf)
            return out.astype(r.dtype)
        return _bi_wkv(r, k, v, w, u, time_emb)

    def _L0_attn_ref(x, Wq, Wk, Wv, Wo, betas):
        import jax, jax.numpy as jnp
        import numpy as np
        B, S, D = (2, 1024, 512)
        H, DK, DV = (16, 128, 128)
        SEG = 128
        UPDATE = 'delta'
        CAUSAL = True
        Bsz, seq, _ = x.shape
        nseg = seq // SEG
        q = (x @ Wq).reshape(Bsz, seq, H, DK).transpose(0, 2, 1, 3)
        k = (x @ Wk).reshape(Bsz, seq, H, DK).transpose(0, 2, 1, 3)
        v = (x @ Wv).reshape(Bsz, seq, H, DV).transpose(0, 2, 1, 3)
        qs = q.reshape(Bsz, H, nseg, SEG, DK).transpose(2, 0, 1, 3, 4)
        ks_ = k.reshape(Bsz, H, nseg, SEG, DK).transpose(2, 0, 1, 3, 4)
        vs = v.reshape(Bsz, H, nseg, SEG, DV).transpose(2, 0, 1, 3, 4)
        causal_mask = jnp.tril(jnp.ones((SEG, SEG), bool))
        scale = DK ** 0.5
        beta = jax.nn.sigmoid(betas)

        def step(carry, seg):
            mem, z = carry
            qq, kk, vv = seg
            sigma_q = jax.nn.elu(qq) + 1.0
            scores = jnp.einsum('bhsk,bhtk->bhst', qq, kk) / scale
            if CAUSAL:
                scores = jnp.where(causal_mask, scores, -jnp.inf)
            att_dot = jax.nn.softmax(scores, axis=-1) @ vv
            att_mem = sigma_q @ mem / (sigma_q @ z)
            sigma_k = jax.nn.elu(kk) + 1.0
            if UPDATE == 'linear':
                mem_new = mem + jnp.einsum('bhsk,bhsv->bhkv', sigma_k, vv)
            else:
                delta = vv - sigma_k @ mem / (sigma_k @ z)
                mem_new = mem + jnp.einsum('bhsk,bhsv->bhkv', sigma_k, delta)
            z_new = z + sigma_k.sum(axis=-2, keepdims=True).transpose(0, 1, 3, 2)
            att = beta * att_mem + (1.0 - beta) * att_dot
            out = att.reshape(Bsz, SEG, H * DV) @ Wo
            return ((mem_new, z_new), out)
        mem0 = jnp.zeros((Bsz, H, DK, DV), x.dtype)
        z0 = jnp.ones((Bsz, H, DK, 1), x.dtype) / DK
        _, outs = jax.lax.scan(step, (mem0, z0), (qs, ks_, vs))
        return outs.transpose(1, 0, 2, 3).reshape(Bsz, seq, D)

    def _L0_cond2_ref(r, k, v, w, u, time_emb):
        import jax, jax.numpy as jnp
        from jax import lax
        import numpy as np
        B, T, C, TD = (8, 512, 512, 128)

        def _bi_wkv(r, k, v, w, u, time_emb):
            tf = jax.nn.sigmoid(jnp.sum(time_emb, axis=-1))[:, None, None]
            decay = jnp.exp(-jnp.exp(w.astype(jnp.float32)))[None, :] * (0.5 + 0.5 * tf[:, :, 0])
            kf = k.astype(jnp.float32)
            vf = v.astype(jnp.float32)
            ek = jnp.exp(jnp.minimum(kf, 30.0))
            ekv = ek * vf

            def step(carry, x):
                a, b = carry
                ekv_t, ek_t = x
                a = a * decay + ekv_t
                b = b * decay + ek_t
                return ((a, b), (a, b))
            ekv_t = jnp.swapaxes(ekv, 0, 1)
            ek_t = jnp.swapaxes(ek, 0, 1)
            init = (jnp.zeros_like(decay), jnp.zeros_like(decay))
            _, (nf, df) = lax.scan(step, init, (ekv_t, ek_t))
            _, (nb, db) = lax.scan(step, init, (ekv_t, ek_t), reverse=True)
            nf = jnp.swapaxes(nf, 0, 1)
            df = jnp.swapaxes(df, 0, 1)
            nb = jnp.swapaxes(nb, 0, 1)
            db = jnp.swapaxes(db, 0, 1)
            euk = jnp.exp(jnp.minimum(u.astype(jnp.float32)[None, None, :] + kf, 30.0))
            num = nf + nb - ekv + euk * vf
            den = df + db - ek + euk
            base = jax.nn.sigmoid(r.astype(jnp.float32)) * (num / jnp.maximum(den, 1e-08))
            out = base * (0.8 + 0.2 * tf)
            return out.astype(r.dtype)
        return _bi_wkv(r, k, v, w, u, time_emb)

    def _L0_ffn_ref(x, W1, W2, W3):
        import jax, jax.numpy as jnp
        import numpy as np
        B, S, D, H = (4, 512, 512, 2048)

        def fwht(x):
            orig_shape = x.shape
            n = orig_shape[-1]
            x = x.reshape(-1, n)
            h = 1
            while h < n:
                xb = x.reshape(-1, n // (2 * h), 2, h)
                a = xb[:, :, 0, :]
                b = xb[:, :, 1, :]
                x = jnp.stack([a + b, a - b], axis=2).reshape(-1, n)
                h *= 2
            scale = jnp.asarray(1.0 / np.sqrt(n), dtype=x.dtype)
            return (x * scale).reshape(orig_shape)
        up_gate = jnp.einsum('bsd,hd->bsh', x, W1)
        up_lin = jnp.einsum('bsd,hd->bsh', x, W3)
        hidden = jax.nn.silu(up_gate) * up_lin
        hidden = fwht(hidden)
        out = jnp.einsum('bsh,dh->bsd', hidden, W2)
        return out
    x = x + _L0_attn_ref(_L0_cond_ref(x, fside_BxSxS_0, fside_BxSxS_0, L0_cond_w, L0_cond_u, cond_512), L0_attn_Wq, L0_attn_Wk, L0_attn_Wv, L0_attn_Wo, L0_attn_betas)
    x = x + _L0_ffn_ref(_L0_cond2_ref(x, fside_BxSxS_0, fside_BxSxS_0, L0_cond2_w, L0_cond2_u, cond_512), L0_ffn_W1, L0_ffn_W2, L0_ffn_W3)
    return x

_drawn_inputs = setup_inputs


def setup_inputs(seed=0):
    import zlib

    import numpy as np

    out = dict(_drawn_inputs(seed))
    spreads = {}
    factors = {'L0_cond_u': 5.732,
     'L0_attn_Wq': 8.0,
     'L0_attn_Wk': 8.0,
     'L0_attn_betas': 3.236,
     'L0_cond2_u': 2.882}
    for name, (base, spread) in spreads.items():
        noise = np.random.default_rng([zlib.crc32(name.encode()), seed]).standard_normal(out[name].shape)
        drawn = base * np.exp(spread * noise) if base else spread * noise
        out[name] = jnp.asarray(drawn.astype(out[name].dtype))
    for name, factor in factors.items():
        out[name] = (out[name] * factor).astype(out[name].dtype)
    return out
```

```python
from contextlib import ExitStack

import concourse.bass as bass
from concourse import mybir

F32 = mybir.dt.float32
F32R = mybir.dt.float32r
ALU = mybir.AluOpType
ACT = mybir.ActivationFunctionType
AX_X = mybir.AxisListType.X

P = 128
NB = 4
T = 512
C = 512
NC = C // P
H = 16
SEG = 128
NSEG = T // SEG
NG = 8
NRING = 6
NSTAGE = 3
HID = 2048
SCALE = float(P) ** -0.5
RSQ = float(HID) ** -0.5
NEG = -3.0e38
PE, DV, AC, PL, SP = "tensor", "vector", "scalar", "gpsimd", "sync"


class Queues:

    def __init__(self, nc, ctx):
        self.nc, self.ctx = nc, ctx
        self.todo = {e: [] for e in (PE, DV, AC, PL, SP)}
        self.sems, self.count, self.seen = {}, {}, {}
        self.last = {}

    def step(self, name, by):
        if name not in self.sems:
            self.sems[name] = self.ctx.enter_context(self.nc.semaphore(name))
            self.count[name] = 0
        self.count[name] += by
        return name, self.count[name]

    def put(self, eng, waits, fn, name=None, by=1):
        need = []
        for n, v in waits:
            if self.seen.get((eng, n), 0) < v:
                self.seen[(eng, n)] = v
                need = [x for x in need if x[0] != n] + [(n, v)]
        mark = self.step(name, by) if name else None
        if mark:
            self.last[(eng, name)] = mark
        self.todo[eng].append((need, fn, name, by))
        return mark

    def dma(self, waits, out, in_, name):
        return self.put(SP, waits, lambda e: e.dma_start(out, in_), name, 16)

    def run(self, block):
        def program(todo):
            def body(e):
                for need, fn, name, by in todo:
                    for n, v in need:
                        e.wait_ge(self.sems[n], v)
                    if fn is None:
                        continue
                    ins = fn(e)
                    if name:
                        ins.then_inc(self.sems[name], by)
            return body
        block.tensor(program(self.todo[PE]))
        block.vector(program(self.todo[DV]))
        block.scalar(program(self.todo[AC]))
        block.gpsimd(program(self.todo[PL]))
        block.sync(program(self.todo[SP]))


def adaln_attn_ffn(nc, xT_d, fT_d, cond_d, wu_d, wq_d, wk_d, wv_d, wo_d, betas_d,
                   w1_d, w3_d, w2_d, ident_d, mask_d, had_d, out_d):
    beta_s = nc.dram_tensor("beta_s", [2, H, P], F32).ap()
    ratio_s = nc.dram_tensor("ratio_s", [NB, NC, P, T], F32).ap()
    x1_s = nc.dram_tensor("x1_s", [NB, P, NC, T], F32).ap()
    w2_s = nc.dram_tensor("w2_s", [8, P, 16, 64], F32).ap()

    with ExitStack() as ctx:
        Q = Queues(nc, ctx)

        def sb(stack, name, shape, dt=F32):
            return stack.enter_context(nc.sbuf_tensor(name, shape, dt))

        banks = {n: ctx.enter_context(nc.psum_tensor("ps" + n, [P, 512], F32))
                 for n in ("G0", "G1", "X0", "X1", "Y0", "Y1", "Z0", "Z1")}

        yh = [sb(ctx, f"yh{i}", [P, NC, T], F32R) for i in range(2)]
        yl = [sb(ctx, f"yl{i}", [P, NC, T], F32R) for i in range(2)]
        wh = [sb(ctx, f"wh{i}", [P, 1024], F32R) for i in range(NRING)]
        wl = [sb(ctx, f"wl{i}", [P, 1024], F32R) for i in range(NRING)]
        stage = [sb(ctx, f"stage{i}", [P, 512]) for i in range(NSTAGE)]
        wu = sb(ctx, "wu", [P, 4, NC])
        ucut = sb(ctx, "ucut", [P, 2, NC])
        dec0 = sb(ctx, "dec0", [P, 2, NC])
        dec = sb(ctx, "dec", [P, NB, 2, NC])
        tf = sb(ctx, "tf", [P, 4, NB])

        two = ExitStack()
        kx = [sb(two, f"kx{i}", [P, T]) for i in range(2)]
        EK, EKV, EU, EUV, NF, DF, ER, OY = (
            sb(two, n, [P, T]) for n in ("EK", "EKV", "EU", "EUV", "NF", "DF", "ER", "OY"))
        NBK = sb(two, "NBK", [P, T + 1])
        DBK = sb(two, "DBK", [P, T + 1])
        two.close()
        three = ExitStack()
        HA, HB, HO = (sb(three, n, [P, 1024]) for n in ("HA", "HB", "HO"))
        HH = sb(three, "HH", [P, 1024], F32R)
        HL = sb(three, "HL", [P, 1024], F32R)
        hadf = sb(three, "hadf", [P, P])
        had = sb(three, "had", [P, P], F32R)
        three.close()
        sg = [sb(ctx, f"sg{i}", [P, T]) for i in range(6)]
        rt = [sb(ctx, f"rt{i}", [P, T]) for i in range(2)]
        hh = [sb(ctx, "hh0", [P, 2, T], F32R)]
        hl = [sb(ctx, "hl0", [P, 2, T], F32R)]
        sb(ctx, "pad", [P, 32])

        one = ExitStack()
        xb = sb(one, "xb", [P, NC, T])
        ah = sb(one, "ah", [P, 16, 256], F32R)
        al = sb(one, "al", [P, 16, 256], F32R)
        qT = sb(one, "qT", [P, 2, T])
        kT = sb(one, "kT", [P, 2, T])
        sq = sb(one, "sq", [P, 2, T])
        sk = sb(one, "sk", [P, 2, T])
        v = [sb(one, f"v{i}", [P, NSEG, 2, P + 1]) for i in range(2)]
        vs = sb(one, "vs", [P, NSEG, 2, P])
        S = sb(one, "S", [P, 2, T])
        pT = sb(one, "pT", [P, 2, T])
        kn = sb(one, "kn", [P, 2, 3, P])
        t2 = sb(one, "t2", [P, 2, 3, P])
        mem = sb(one, "mem", [P, 2, P + 1])
        mem0 = sb(one, "mem0", [P, P + 1])
        delta = sb(one, "delta", [P, 2, P + 1])
        bet = sb(one, "bet", [P, 256])
        omb = sb(one, "omb", [P, 256])
        etmp = sb(one, "etmp", [P, T])
        ident = sb(one, "ident", [P, P])
        mask = sb(one, "mask", [P, P])
        st = sb(one, "st", [P, 4, 2, NSEG])
        rz = sb(one, "rz", [P, 2, 2])
        one.close()
        x = sb(ctx, "x", [P, NB, NC, T])
        zh = yh + [sb(ctx, f"zh{i}", [P, NC, T], F32R) for i in (2, 3)]
        zl = yl + [sb(ctx, f"zl{i}", [P, NC, T], F32R) for i in (2, 3)]
        hh += [sb(ctx, "hh1", [P, 2, T], F32R)]
        hl += [sb(ctx, "hl1", [P, 2, T], F32R)]

        cb = S[:, 0, :]
        bt = S[0:H, 1, 0:P]
        m_wu = Q.dma([], wu[:, :, :], wu_d, "d_wu")
        m_cb = Q.dma([], cb, cond_d.to_broadcast([P, NB * P]), "d_cb")
        m_kx = {}
        for i in range(2):
            m_kx[i] = Q.dma([], kx[i][:, :], fT_d[0, :, i, :], f"d_k{i}")
        m_er = {0: Q.dma([], ER[:, :], xT_d[0, :, 0, :], "d_er")}
        m_xb = {0: Q.dma([], xb[:, :, :], xT_d[0], "d_xb")}
        m_bt = Q.dma([], bt, betas_d, "d_bt")
        m_id = Q.dma([], ident[:, :], ident_d, "d_id")
        m_mk = Q.dma([], mask[:, :], mask_d, "d_mk")

        e_w = Q.put(AC, [m_wu], lambda e: e.activation(dec0[:, :, :], wu[:, 0:4:2, :], ACT.Exp), "a_c")
        e_w = Q.put(AC, [e_w], lambda e: e.activation(dec0[:, :, :], dec0[:, :, :], ACT.Exp, scale=-1.0), "a_c")
        c1 = Q.put(DV, [m_cb], lambda e: e.tensor_reduce(
            tf[:, 0, :], cb.rearrange("p (b t) -> p b t", b=NB), AX_X, ALU.add), "v_c")
        e_t = Q.put(AC, [c1], lambda e: e.activation(tf[:, 1, :], tf[:, 0, :], ACT.Exp, scale=-1.0), "a_c")
        c1 = Q.put(DV, [e_t], lambda e: e.tensor_scalar_add(tf[:, 1, :], tf[:, 1, :], 1.0), "v_c")
        c1 = Q.put(DV, [c1], lambda e: e.reciprocal(tf[:, 0, :], tf[:, 1, :]), "v_c")
        c1 = Q.put(DV, [c1], lambda e: e.tensor_scalar(tf[:, 1, :], tf[:, 0, :], 0.5, 0.5, ALU.mult, ALU.add), "v_c")
        m_s = Q.put(DV, [c1], lambda e: e.tensor_scalar(tf[:, 2, :], tf[:, 0, :], 0.2, 0.8, ALU.mult, ALU.add), "v_c")
        for b in range(NB):
            m_dec = Q.put(DV, [c1, m_s, e_w], lambda e, b=b: e.tensor_scalar(
                dec[:, b, :, :], dec0[:, :, :], tf[:, 1, b:b + 1], None, ALU.mult), "v_c")
        m_cut = Q.put(DV, [m_wu], lambda e: e.tensor_scalar(
            ucut[:, :, :], wu[:, 1:4:2, :], -1.0, 30.0, ALU.mult, ALU.add), "v_c")
        m_nb0 = Q.put(DV, [], lambda e: e.memset(NBK[:, T:T + 1], 0.0), "v_c")
        m_nb0 = Q.put(DV, [], lambda e: e.memset(DBK[:, T:T + 1], 0.0), "v_c")

        def early_constants():
            e_b = Q.put(AC, [m_bt], lambda e: e.activation(bt, bt, ACT.Exp, scale=-1.0), "a_c")
            c = Q.put(DV, [e_b], lambda e: e.tensor_scalar_add(bt, bt, 1.0), "v_c")
            c = Q.put(DV, [c], lambda e: e.reciprocal(S[0:H, 1, P:2 * P], bt), "v_c")
            c = Q.put(DV, [c], lambda e: e.tensor_scalar(
                S[0:H, 1, 2 * P:3 * P], S[0:H, 1, P:2 * P], -1.0, 1.0, ALU.mult, ALU.add), "v_c")
            a = Q.dma([c], beta_s[0], S[0:H, 1, P:2 * P], "d_b0")
            b = Q.dma([c], beta_s[1], S[0:H, 1, 2 * P:3 * P], "d_b1")
            for t in v:
                Q.put(DV, [], lambda e, t=t: e.memset(t[:, :, :, P:P + 1], 1.0), "v_c")
            Q.put(DV, [], lambda e: e.memset(mem0[:, 0:P], 0.0), "v_c")
            Q.put(DV, [], lambda e: e.memset(mem0[:, P:P + 1], 1.0 / P), "v_c")
            d = Q.put(DV, [], lambda e: e.memset(delta[:, :, P:P + 1], 1.0), "v_c")
            return a, b, d

        order = [(g, b) for b in range(NB) for g in range(NG)]
        stream, windex = [], {}

        def streamed(k, g, key):
            windex[k, key] = len(stream)
            stream.append((k, g))

        for n in range(-1, len(order)):
            if n >= 0 and n % 4 == 0 and n > 0:
                for i in range(8):
                    streamed("o", i, (n - 1, i))
            if n + 1 < len(order):
                for k in "vkq":
                    streamed(k, order[n + 1][0], n + 1)
        for i in range(8):
            streamed("o", i, (len(order) - 1, i))
        for g in range(NG):
            for k in "132":
                streamed(k, g, g)
        src = {"q": wq_d, "k": wk_d, "v": wv_d, "o": wo_d, "1": w1_d, "3": w3_d}
        W = {"next": 0, "load": 0, "split": 0, "half": [], "ready": {}, "used": {}}
        stage_free = [[] for _ in range(NSTAGE)]
        m_w2s = []

        def load_halves():
            while W["load"] < 2 * len(stream) and W["load"] < W["split"] + NSTAGE:
                i, half = divmod(W["load"], 2)
                k, g = stream[i]
                if k == "2" and not m_w2s:
                    return
                s = W["load"] % NSTAGE
                if k == "2":
                    out = stage[s][:, :].rearrange("p (n a d) -> p n a d", n=4, a=2)
                    in_ = w2_s[4 * half:4 * half + 4, :, 2 * g:2 * g + 2, :].rearrange("n p a d -> p n a d")
                    m = Q.dma(stage_free[s] + m_w2s, out, in_, f"d_w{s}")
                else:
                    m = Q.dma(stage_free[s], stage[s][:, :], src[k][g, :, half, :], f"d_w{s}")
                W["half"].append(m)
                W["load"] += 1

        def split_weights(limit=1):
            n = 0
            while W["next"] < len(stream) and n < limit:
                i = W["next"]
                k = stream[i][0]
                if i >= NRING and (i - NRING) not in W["used"]:
                    return
                load_halves()
                if W["load"] < 2 * i + 2 and k == "2" and not m_w2s:
                    return
                slot = i % NRING
                free = W["used"].get(i - NRING, [])
                marks = []
                for half in range(2):
                    s = (2 * i + half) % NSTAGE
                    m_in = W["half"][2 * i + half]
                    if k == "2":
                        hi = wh[slot][:, :].rearrange("p (a n d) -> p n a d", a=2, n=8)[:, 4 * half:4 * half + 4]
                        lo = wl[slot][:, :].rearrange("p (a n d) -> p n a d", a=2, n=8)[:, 4 * half:4 * half + 4]
                        raw = stage[s][:, :].rearrange("p (n a d) -> p n a d", n=4, a=2)
                    else:
                        hi = wh[slot][:, 512 * half:512 * half + 512]
                        lo = wl[slot][:, 512 * half:512 * half + 512]
                        raw = stage[s][:, :]
                    a = Q.put(PL, [m_in] + free, lambda e, hi=hi, raw=raw: e.tensor_scalar(
                        hi, raw, 1.0, 0.0, ALU.mult, ALU.add), "p_wh")
                    p = Q.put(PL, [a, m_in] + free, lambda e, lo=lo, raw=raw, hi=hi: e.tensor_tensor(
                        lo, raw, hi, ALU.subtract), "p_wl")
                    stage_free[s] = [a, p]
                    marks += [a, p]
                    W["split"] += 1
                    load_halves()
                    if half == 0 and W["load"] < 2 * i + 2:
                        raise AssertionError("a weight's second half is not there")
                W["next"] = i + 1
                W["ready"][i] = marks
                n += 1

        bank_free = {n: [] for n in banks}

        def passes(bank, out, terms, waits, name, part=(0, 1), free=True):
            k, n = part
            if free and k == 0:
                waits = waits + bank_free[bank]
            pairs = [p for (lh, ll), (rh, rl) in terms for p in ((lh, rh), (lh, rl), (ll, rh))]
            first, end = k * len(pairs) // n, (k + 1) * len(pairs) // n
            for i in range(first, end):
                a, c = pairs[i]
                m = Q.put(PE, waits if i == first else [], lambda e, a=a, c=c, i=i: e.matmul(
                    out, a, c, start=(i == 0), stop=(i == len(pairs) - 1)), name if i == len(pairs) - 1 else None)
            return m

        y_ready = {}
        y_free = {0: [], 1: []}
        tiles = [(i, b, c) for i, b in ((0, 0), (0, 1), (1, 0), (0, 2), (1, 1), (0, 3), (1, 2), (1, 3)) for c in range(NC)]
        B = {"EK": [], "EU": [], "N": [], "kfree": {0: [], 1: []}, "ER": [], "OY": []}
        m_ratio = {}
        A = {n: {} for n in range(len(tiles) + 1)}
        firsts = [n for n, t in enumerate(tiles) if t[0] == 0]

        def k_load(n):
            if 2 <= n < len(tiles):
                _, b, c = tiles[n]
                m_kx[n] = Q.dma(B["kfree"][n % 2], kx[n % 2][:, :], fT_d[b, :, c, :], f"d_k{n % 2}")

        def er_load(n):
            if n in firsts and n > 0:
                _, b, c = tiles[n]
                m_er[n] = Q.dma(B["ER"], ER[:, :], xT_d[b, :, c, :], "d_er")

        def a_min(n):
            if n < len(tiles):
                k = kx[n % 2][:, :]
                A[n]["mn"] = Q.put(DV, [m_kx[n]] + B["EK"], lambda e: e.tensor_scalar(EK[:, :], k, 30.0, None, ALU.min), "v_sc")

        def a_exp(n):
            if n < len(tiles):
                A[n]["ek"] = Q.put(AC, [A[n]["mn"]], lambda e: e.activation(EK[:, :], EK[:, :], ACT.Exp), "a_ek")

        def a_mul(n):
            if n < len(tiles):
                k = kx[n % 2][:, :]
                A[n]["ekv"] = Q.put(PL, [A[n]["ek"]] + B["EK"], lambda e: e.tensor_tensor(EKV[:, :], EK[:, :], k, ALU.mult), "p_ekv")

        def b_min(n):
            if n < len(tiles):
                k, (i, b, c) = kx[n % 2][:, :], tiles[n]
                A[n]["mu"] = Q.put(DV, [m_kx[n], m_cut] + B["EU"], lambda e: e.tensor_scalar(
                    EU[:, :], k, ucut[:, i, c:c + 1], None, ALU.min), "v_sc")

        def b_exp(n):
            if n < len(tiles):
                i, b, c = tiles[n]
                A[n]["eu"] = Q.put(AC, [A[n]["mu"]], lambda e: e.activation(
                    EU[:, :], EU[:, :], ACT.Exp, bias=wu[:, 2 * i + 1, c:c + 1]), "a_eu")

        def b_mul(n):
            if n < len(tiles):
                k = kx[n % 2][:, :]
                A[n]["euv"] = Q.put(PL, [A[n]["eu"]] + B["EU"], lambda e: e.tensor_tensor(EUV[:, :], EU[:, :], k, ALU.mult), "p_euv")
                B["kfree"][n % 2] = [A[n]["euv"], A[n]["ekv"]]

        def e_exp(n):
            if n in firsts:
                A[n]["er"] = Q.put(AC, [m_er[n]], lambda e: e.activation(ER[:, :], ER[:, :], ACT.Exp, scale=-1.0), "a_er")

        def scan_steps(n):
            i, b, c = tiles[n]
            d = dec[:, b, i, c:c + 1]
            db = d.to_broadcast([P, T])
            M = {}
            after = ([f for f in firsts if f > n] or [None])[0]

            def s1():
                k_load(n + 2)
                M["nf"] = Q.put(DV, [A[n]["ekv"], m_dec] + B["N"], lambda e: e.tensor_tensor_scan(
                    NF[:, :], db, EKV[:, :], 0.0, ALU.mult, ALU.add), "v_sc")

            def s2():
                M["nb"] = Q.put(DV, [A[n]["ekv"]], lambda e: e.tensor_tensor_scan(
                    NBK[:, T - 1::-1], db, EKV[:, ::-1], 0.0, ALU.mult, ALU.add), "v_sc")

            def s3():
                M["df"] = Q.put(DV, [A[n]["ek"]], lambda e: e.tensor_tensor_scan(
                    DF[:, :], db, EK[:, :], 0.0, ALU.mult, ALU.add), "v_sc")

            def s4():
                M["db"] = Q.put(DV, [A[n]["ek"]], lambda e: e.tensor_tensor_scan(
                    DBK[:, T - 1::-1], db, EK[:, ::-1], 0.0, ALU.mult, ALU.add), "v_sc")
                B["EK"] = [M["db"]]

            def n1():
                M["n"] = Q.put(DV, [M["nb"], m_nb0], lambda e: e.scalar_tensor_tensor(
                    NF[:, :], NBK[:, 1:T + 1], d, NF[:, :], ALU.mult, ALU.add), "v_sc")

            def n2():
                M["n"] = Q.put(DV, [M["n"], A[n]["euv"]], lambda e: e.tensor_tensor(
                    NF[:, :], NF[:, :], EUV[:, :], ALU.add), "v_sc")

            def d1():
                M["d"] = Q.put(DV, [M["db"]], lambda e: e.scalar_tensor_tensor(
                    DF[:, :], DBK[:, 1:T + 1], d, DF[:, :], ALU.mult, ALU.add), "v_sc")

            def d2():
                M["d"] = Q.put(DV, [M["d"], A[n]["eu"]], lambda e: e.tensor_tensor(
                    DF[:, :], DF[:, :], EU[:, :], ALU.add), "v_sc")
                B["EU"] = [M["d"]]

            def d3():
                M["d"] = Q.put(DV, [M["d"]], lambda e: e.tensor_scalar(
                    DF[:, :], DF[:, :], 1e-8, None, ALU.max), "v_sc")

            def d4():
                if i == 0:
                    M["d"] = Q.put(DV, [M["d"], A[n]["er"]], lambda e: e.scalar_tensor_tensor(
                        DF[:, :], ER[:, :], 1.0, DF[:, :], ALU.add, ALU.mult), "v_sc")
                    B["ER"] = [M["d"]]

            def rc(j):
                M["r"] = Q.put(DV, [M["d"]], lambda e: e.reciprocal(
                    DBK[:, 128 * j:128 * j + 128], DF[:, 128 * j:128 * j + 128]), "v_sc")
                if j == 1 and i == 0 and after is not None:
                    er_load(after)

            def out():
                M["o"] = Q.put(DV, [M["r"]] + B["OY"], lambda e: e.scalar_tensor_tensor(
                    OY[:, :], NF[:, :], tf[:, 2, b:b + 1], DBK[:, 0:T], ALU.mult, ALU.mult), "v_sc")
                B["N"] = [M["o"]]

            def store():
                m = M["o"]
                if i == 0:
                    s = b % 2
                    free = y_free.get(b, [])
                    h = Q.put(AC, [m] + free, lambda e: e.activation(yh[s][:, c, :], OY[:, :], ACT.Copy), "a_yh")
                    l = Q.put(PL, [h, m] + free, lambda e: e.tensor_tensor(
                        yl[s][:, c, :], OY[:, :], yh[s][:, c, :], ALU.subtract), "p_yl")
                    y_ready.setdefault(b, []).extend([h, l])
                    B["OY"] = [l, h]
                    if after is not None:
                        e_exp(after)
                else:
                    s = Q.dma([m], ratio_s[b, c], OY[:, :], "d_rs")
                    m_ratio[b, c] = s
                    B["OY"] = [s]

            N = n + 1
            return [(600, s1), (600, s2), (600, s3), (600, s4), (335, lambda: a_min(N)), (660, n1), (600, n2),
                    (0, lambda: a_exp(N)), (660, d1), (600, d2), (335, lambda: b_min(N)), (0, lambda: a_mul(N)),
                    (335, d3), (660 if i == 0 else 0, d4), (0, lambda: b_exp(N)), (880, lambda: rc(0)),
                    (880, lambda: rc(1)), (0, lambda: b_mul(N)), (880, lambda: rc(2)), (880, lambda: rc(3)),
                    (700, out), (0, store)]

        def had_steps():
            M = {}

            def first():
                bar = [Q.last[DV, "v_sc"], Q.last[PL, "p_ekv"], Q.last[PL, "p_euv"], Q.last[AC, "a_eu"],
                       Q.last[AC, "a_ek"], Q.last[AC, "a_yh"], Q.last[AC, "a_er"], Q.last[SP, "d_rs"],
                       Q.last[PL, "p_yl"]]
                M["ha"] = bar
                M["out"] = bar
                M["hb"] = bar
                d = Q.dma(bar, hadf[:, :], had_d, "d_had")
                M["had"] = Q.put(AC, [d], lambda e: e.activation(had[:, :], hadf[:, :], ACT.Copy), "a_had")
                M["load"] = Q.dma(bar, HA[:, :], w2_d[0].rearrange("p a d -> p (a d)"), "d_h")

            def level(lv):
                w = 64 << lv
                a = [HA, HB][lv % 2][:, :].rearrange("p (x t w) -> p x t w", t=2, w=w)
                o = [HB, HA][lv % 2][:, :].rearrange("p (x t w) -> p x t w", t=2, w=w)
                waits = [M["load"]] if lv == 0 else [M["lv"]]
                if lv == 0:
                    waits = waits + M["hb"]
                Q.put(PL, waits, lambda e: e.tensor_tensor(
                    o[:, :, 0, :], a[:, :, 0, :], a[:, :, 1, :], ALU.add), "p_h")
                M["lv"] = Q.put(PL, [], lambda e: e.tensor_tensor(
                    o[:, :, 1, :], a[:, :, 0, :], a[:, :, 1, :], ALU.subtract), "p_h")

            def parts():
                M["hi"] = Q.put(AC, [M["lv"]] + M.get("pe", M["ha"]), lambda e: e.activation(HH[:, :], HA[:, :], ACT.Copy), "a_h")
                M["lo"] = Q.put(PL, [M["hi"]], lambda e: e.tensor_tensor(HL[:, :], HA[:, :], HH[:, :], ALU.subtract), "p_h")
                M["hb"] = [M["lo"]]

            def mult(n):
                if n + 1 < 8:
                    M["load"] = Q.dma([M["lo"], M["hi"]], HA[:, :], w2_d[n + 1].rearrange("p a d -> p (a d)"), "d_h")
                for j in range(2):
                    bank = next_g()
                    bk = banks[bank]
                    cut = slice(512 * j, 512 * j + 512)
                    Q.put(PE, bank_free[bank] + [M["had"], M["hi"], M["lo"]], lambda e, bk=bk, cut=cut: e.matmul(
                        bk[:, :], had[:, :], HH[:, cut], start=True, stop=False))
                    m = Q.put(PE, [], lambda e, bk=bk, cut=cut: e.matmul(
                        bk[:, :], had[:, :], HL[:, cut], start=False, stop=True), "pe_h")
                    M["pe"] = [m]
                    o = Q.put(AC, [m] + M["out"], lambda e, bk=bk, cut=cut: e.activation(
                        HO[:, cut], bk[:, :], ACT.Copy, scale=RSQ), "a_ho")
                    bank_free[bank] = [o]
                M["out"] = [Q.dma([o], w2_s[n].rearrange("p a d -> p (a d)"), HO[:, :], "d_ho")]
                if n == 7:
                    m_w2s[:] = M["out"]

            steps = [(0, first)]
            for n in range(8):
                steps += [(500, lambda lv=lv: level(lv)) for lv in range(4)]
                steps += [(500, parts), (0, None), (0, lambda n=n: mult(n))]
            return steps

        gi = [0]

        def next_g():
            gi[0] += 1
            return f"G{gi[0] % 2}"

        background = []
        for n in range(len(tiles)):
            background += [(cost, fn, n) for cost, fn in scan_steps(n)]
        background += [(cost, fn, len(tiles)) for cost, fn in had_steps()]
        at = [0]
        whole = [False]

        def work(ns):
            while ns > 0 and at[0] < len(background):
                cost, fn, tile = background[at[0]]
                if tile < len(tiles) and tiles[tile][0] == 0 and tiles[tile][1] not in y_free:
                    return
                if fn is None and not whole[0]:
                    return
                at[0] += 1
                if fn is not None:
                    fn()
                ns -= max(cost, 1)

        def work_until(tile):
            while at[0] < len(background) and background[at[0]][2] <= tile:
                fn = background[at[0]][1]
                at[0] += 1
                if fn is not None:
                    fn()

        D = {}

        def kq(n, which, j, part):
            g, b = order[n]
            wi = windex[which, n]
            slot, ys = wi % NRING, b % 2
            if part == 0:
                D["bank"] = next_g()
            bank = D["bank"]
            terms = [((wh[slot][:, 256 * c + 128 * j:256 * c + 128 * j + 128],
                       wl[slot][:, 256 * c + 128 * j:256 * c + 128 * j + 128]),
                      (yh[ys][:, c, :], yl[ys][:, c, :])) for c in range(NC)]
            m = passes(bank, banks[bank][:, :], terms, W["ready"][wi] + y_ready[b], "pe_g", part=(part, 2))
            if part == 0:
                return
            if j == 1:
                W["used"][wi] = [m]
                if g == NG - 1 and which == "q":
                    y_free[b + 2] = [m]
            dst, sig = (qT, sq) if which == "q" else (kT, sk)
            a = Q.put(AC, [m] + D.get("scores", []), lambda e: e.activation(dst[:, j, :], banks[bank][:, :], ACT.Copy), "a_qk")
            bank_free[bank] = [a]
            D[which, j] = a
            p = Q.put(AC, [m] + D.get("etmp", []), lambda e: e.activation(
                etmp[:, :], banks[bank][:, :], ACT.Relu, scale=-1.0), "a_mn")
            bank_free[bank] = [p]
            x2 = Q.put(AC, [p], lambda e: e.activation(etmp[:, :], etmp[:, :], ACT.Exp, scale=-1.0), "a_e")
            old = D.get("am3" if which == "q" else "dk2", [])
            s = Q.put(DV, [x2, a] + old, lambda e: e.scalar_tensor_tensor(
                sig[:, j, :], dst[:, j, :], 1.0, etmp[:, :], ALU.add, ALU.max), "v_sg")
            D["etmp"] = [s]
            D["s" + which, j] = s

        def vv(n, half, part):
            g, b = order[n]
            wi = windex["v", n]
            slot, ys = wi % NRING, b % 2
            if part == 0:
                D["bank"] = next_g()
            bank = D["bank"]
            bk = banks[bank]
            t = 2 * half + part
            terms = [((yh[ys][:, c, 128 * t:128 * t + 128], yl[ys][:, c, 128 * t:128 * t + 128]),
                      (wh[slot][:, 256 * c:256 * c + 256], wl[slot][:, 256 * c:256 * c + 256])) for c in range(NC)]
            m = passes(bank, bk[:, 256 * part:256 * part + 256], terms, W["ready"][wi] + y_ready[b], "pe_g", free=(part == 0))
            if part == 0:
                return
            if half == 1:
                W["used"][wi] = [m]
            vt = v[n % 2]
            a = Q.put(AC, [m] + D.get(("u2", n - 2), []), lambda e: e.activation(
                vt[:, 2 * half:2 * half + 2, :, 0:P], bk[:, :].rearrange("p (t h d) -> p t h d", t=2, h=2), ACT.Copy), "a_v")
            bank_free[bank] = [a]
            D["v", n, half] = a

        def v_scaled(n):
            load_omb(n)
            vt = v[n % 2]
            for j in range(2):
                m = Q.put(PL, [D["v", n, 0], D["v", n, 1], D["omb"]] + D.get("pv", []), lambda e, j=j: e.tensor_tensor(
                    vs[:, :, j, :], vt[:, :, j, 0:P],
                    omb[:, 128 * j:128 * j + 128].rearrange("p (a d) -> p a d", a=1).to_broadcast([P, NSEG, P]),
                    ALU.mult), "p_vs")
            D["vs"] = m

        def load_omb(n):
            g = order[n][0]
            if True:
                w = [D["vs"]] if "vs" in D else []
                D["omb"] = Q.dma(w + [m_beta[1]], omb[:, :],
                                 beta_s[1, 2 * g:2 * g + 2, :].rearrange("(o h) d -> o (h d)", o=1).to_broadcast([P, 256]), "d_om")

        def load_bet(n):
            g = order[n][0]
            if True:
                w = D.get("t2_3", [])
                D["bet"] = Q.dma(w + [m_beta[0]], bet[:, :],
                                 beta_s[0, 2 * g:2 * g + 2, :].rearrange("(o h) d -> o (h d)", o=1).to_broadcast([P, 256]), "d_be")

        def wo(n, i):
            wi = windex["o", (n, i)]
            slot = wi % NRING
            if i == 0:
                D["wo_banks"] = [next_g(), next_g()]
            for dc in range(NC):
                bank = D["wo_banks"][dc // 2]
                out = banks[bank][:, 256 * (dc % 2):256 * (dc % 2) + 256]
                pairs = []
                for jj in range(2):
                    lo = 512 * jj + 128 * dc
                    j = 2 * i + jj
                    pairs += [(wh[slot][:, lo:lo + 128], ah[:, j, :]), (wh[slot][:, lo:lo + 128], al[:, j, :]),
                              (wl[slot][:, lo:lo + 128], ah[:, j, :])]
                for k, (a, c) in enumerate(pairs):
                    start = i == 0 and k == 0 and dc % 2 == 0
                    stop = i == 7 and k == 5
                    w = (W["ready"][wi] + D["att"] + bank_free[bank]) if k == 0 else []
                    m = Q.put(PE, w, lambda e, a=a, c=c, out=out, start=start, stop=stop: e.matmul(
                        out, a, c, start=start, stop=stop, skip_group_check=True), "pe_o" if k == 5 else None)
                if i == 7 and dc % 2 == 1:
                    D["wo_done", dc // 2] = m
            W["used"][wi] = [m]
            if i < 7:
                return
            D["wo"] = [m]
            b, half = order[n][1], (n % 8) // 4
            for dc in range(NC):
                bank = D["wo_banks"][dc // 2]
                src_ = banks[bank][:, 256 * (dc % 2):256 * (dc % 2) + 256].rearrange("p (h s r) -> p h s r", h=8, s=4)
                dst = xb[:, dc, :].rearrange("p (s h r) -> p h s r", s=4, h=16)[:, 8 * half:8 * half + 8]
                a = Q.put(DV, [D["wo_done", dc // 2], m_xb[b]], lambda e, src_=src_, dst=dst: e.tensor_tensor(
                    dst, dst, src_, ALU.add), "v_x")
                bank_free[bank] = [a]
            if half == 1:
                m_x1[b] = Q.dma([a], x1_s[b], xb[:, :, :], "d_x1")
                if b + 1 < NB:
                    m_xb[b + 1] = Q.dma([m_x1[b]], xb[:, :, :], xT_d[b + 1], "d_xb")

        m_x1 = {}

        def seg(s):
            return slice(SEG * s, SEG * s + SEG)

        def s1(n):
            for j in range(2):
                bk = banks[f"Y{j}"]
                for s in range(3):
                    m = Q.put(PE, ([D["sk", j], m_id] + bank_free[f"Y{j}"]) if s == 0 else [], lambda e, j=j, s=s, bk=bk: e.transpose(
                        bk[:, seg(s)], sk[:, j, seg(s)], ident[:, :]), "pe_kt" if s == 2 else None)
                a = Q.put(AC, [m] + D.get(("u2", n - 1), []), lambda e, j=j, bk=bk: e.activation(
                    kn[:, j, :, :], bk[:, 0:384].rearrange("p (s k) -> p s k", s=3), ACT.Copy), "a_kn")
                D["kn", j] = a
                bank_free[f"Y{j}"] = [a]
            for j in range(2):
                bk = banks[f"X{j}"]
                for s in range(NSEG):
                    m = Q.put(PE, ([D["q", j], D["k", j]] + bank_free[f"X{j}"]) if s == 0 else [], lambda e, j=j, s=s, bk=bk: e.matmul(
                        bk[:, seg(s)], qT[:, j, seg(s)], kT[:, j, seg(s)], start=True, stop=True), "pe_s" if s == 3 else None)
                D["scores"] = [m]
                for s in range(NSEG):
                    w = [m, m_mk] + D.get("at", []) + list(m_beta[0:2])
                    t = Q.put(DV, w if s == 0 else [], lambda e, j=j, s=s, bk=bk: e.tensor_tensor_reduce(
                        S[:, j, seg(s)], bk[:, seg(s)], mask[:, :], 1.0, NEG, ALU.add, ALU.max,
                        st[:, 0, j, s:s + 1]), "v_mx")
                bank_free[f"X{j}"] = [t]
                t = Q.put(DV, [t] + D.get(("exp", j), []), lambda e, j=j: e.tensor_scalar(
                    st[:, 1, j, :], st[:, 0, j, :], -SCALE, None, ALU.mult), "v_mx")
                for s in range(NSEG):
                    a = Q.put(AC, [t] + D.get("rd", []), lambda e, j=j, s=s: e.activation(
                        S[:, j, seg(s)], S[:, j, seg(s)], ACT.Exp, bias=st[:, 1, j, s:s + 1], scale=SCALE,
                        accum_out=st[:, 2, j, s:s + 1]), "a_p")
                D["exp", j] = [a]

        def update(n, s):
            for j in range(2):
                bk = banks[f"Z{j}"]
                rhs = v[n % 2][:, 0, j, :] if s == 0 else delta[:, j, :]
                w = [D["kn", j], m_beta[2]] + ([D["v", n, 0]] if s == 0 else [D["delta", j]])
                m = Q.put(PE, w + bank_free[f"Z{j}"], lambda e, j=j, bk=bk, rhs=rhs: e.matmul(
                    bk[:, 258:387], kn[:, j, s, :], rhs, start=True, stop=True), "pe_u")
                prev = mem0[:, :] if s == 0 else mem[:, j, :]
                t = Q.put(DV, [m] + D.get("am", []) + D.get(("mem", j), []), lambda e, j=j, bk=bk, prev=prev: e.tensor_tensor(
                    mem[:, j, :], bk[:, 258:387], prev, ALU.add), "v_mem")
                bank_free[f"Z{j}"] = [t]
                D["mem", j] = [t]
            if s == 2:
                D["u2", n] = [m]

        def recall(n, s):
            for j in range(2):
                bk = banks[f"Z{j}"]
                w = bank_free[f"Z{j}"] + D["mem", j] + [D["sq", j]]
                if s < 3:
                    Q.put(PE, w, lambda e, j=j, bk=bk: e.matmul(
                        bk[:, 0:129], sk[:, j, seg(s)], mem[:, j, :], start=True, stop=True))
                m = Q.put(PE, w, lambda e, j=j, bk=bk: e.matmul(
                    bk[:, 129:258], sq[:, j, seg(s)], mem[:, j, :], start=True, stop=True), "pe_am")
                lo = 0 if s < 3 else 1
                t = Q.put(DV, [m] + D.get(("rz", j), []), lambda e, j=j, bk=bk, lo=lo: e.reciprocal(
                    rz[:, j, lo:2], bk[:, 128 + 129 * lo:258:129]), "v_r")
                r = t
                if s < 3:
                    t = Q.put(DV, [r, D["v", n, 0], D["v", n, 1]], lambda e, j=j, bk=bk: e.scalar_tensor_tensor(
                        delta[:, j, 0:P], bk[:, 0:128], rz[:, j, 0:1], v[n % 2][:, s, j, 0:P], ALU.mult, ALU.subtract,
                        reverse1=True), "v_r")
                    D["delta", j] = t
                t = Q.put(DV, [r, D["bet"]], lambda e, j=j, bk=bk: e.scalar_tensor_tensor(
                    t2[:, j, s - 1, :], bk[:, 129:257], rz[:, j, 1:2], bet[:, 128 * j:128 * j + 128],
                    ALU.mult, ALU.mult), "v_r")
                bank_free[f"Z{j}"] = [t]
                D["rz", j] = [t]
                D["t2", j, s] = t
            D["am"] = [m]
            if s == 3:
                D["am3"] = [m]
                D["t2_3"] = [t]
            if s == 2:
                D["dk2"] = [m]

        def turn_p(n):
            for j in range(2):
                bk = banks[f"Y{j}"]
                for s in range(NSEG):
                    m = Q.put(PE, (D["exp", j] + [m_id] + bank_free[f"Y{j}"]) if s == 0 else [], lambda e, j=j, s=s, bk=bk: e.transpose(
                        bk[:, seg(s)], S[:, j, seg(s)], ident[:, :]), "pe_pt" if s == 3 else None)
                a = Q.put(AC, [m] + D.get("pv", []), lambda e, j=j, bk=bk: e.activation(
                    pT[:, j, :], bk[:, :], ACT.Copy), "a_pt")
                D["pT", j] = a
                D["p_read", j] = m
                bank_free[f"Y{j}"] = [a]
            D["rd"] = [Q.put(DV, D["exp", 1] + D["exp", 0], lambda e: e.reciprocal(
                st[:, 3, :, :], st[:, 2, :, :]), "v_rd")]

        def pv(n):
            for j in range(2):
                bk = banks[f"X{j}"]
                for s in range(NSEG):
                    m = Q.put(PE, ([D["pT", j], D["vs"]] + bank_free[f"X{j}"]) if s == 0 else [], lambda e, j=j, s=s, bk=bk: e.matmul(
                        bk[:, seg(s)], pT[:, j, seg(s)], vs[:, s, j, :], start=True, stop=True), "pe_pv" if s == 3 else None)
                D["ad", j] = m
            D["pv"] = [m]

        def join(n, s):
            for j in range(2):
                bk = banks[f"X{j}"]
                w = [D["ad", j], D["p_read", j]] + D["rd"]
                if s == 0:
                    t = Q.put(DV, w, lambda e, j=j, bk=bk: e.tensor_scalar(
                        S[:, j, seg(0)], bk[:, seg(0)], st[:, 3, j, 0:1], None, ALU.mult), "v_at")
                else:
                    t = Q.put(DV, w + [D["t2", j, s]], lambda e, j=j, bk=bk: e.scalar_tensor_tensor(
                        S[:, j, seg(s)], bk[:, seg(s)], st[:, 3, j, s:s + 1], t2[:, j, s - 1, :],
                        ALU.mult, ALU.add), "v_at")
                bank_free[f"X{j}"] = [t]
                D["join", j] = t

        def turn_att(n):
            if n % 4 == 0:
                D["att"] = []
            for j in range(2):
                bk = banks[f"Y{j}"]
                for s in range(NSEG):
                    m = Q.put(PE, ([D["join", j]] + bank_free[f"Y{j}"]) if s == 0 else [], lambda e, j=j, s=s, bk=bk: e.transpose(
                        bk[:, seg(s)], S[:, j, seg(s)], ident[:, :]), "pe_at" if s == 3 else None)
                D["at"] = [m]
                h = 2 * (n % 4) + j
                turned = bk[:, :].rearrange("p (s j) -> p j s", j=16)
                hi, lo = ah[:, :, 32 * h:32 * h + 32], al[:, :, 32 * h:32 * h + 32]
                a = Q.put(AC, [m] + D.get("wo", []), lambda e, hi=hi, turned=turned: e.activation(hi, turned, ACT.Copy), "a_at")
                t = Q.put(DV, [a], lambda e, hi=hi, lo=lo, turned=turned: e.tensor_tensor(lo, turned, hi, ALU.subtract), "v_al")
                bank_free[f"Y{j}"] = [t]
                D["att"] = D["att"] + [a, t]

        z_ready = {}
        F = {}
        rt_free, sg_free = {}, {}

        def modulate(b):
            if not z_ready:
                bar = [Q.last[PL, "p_h"], Q.last[AC, "a_ho"], Q.last[PE, "pe_h"], Q.last[AC, "a_h"], Q.last[SP, "d_ho"]]
                rt_free.update({i: bar for i in range(2)})
                sg_free.update({i: bar for i in range(6)})
            bar = list(Q.last.values()) if b >= 2 else y_free[b + 4 if b == 1 else 4]
            z_ready[b] = []
            marks = []
            for c in range(NC):
                s = c % 2
                m = Q.dma(rt_free[s] + [m_ratio[b, c]], rt[s][:, :], ratio_s[b, c], f"d_rt{s}")
                l = Q.dma(sg_free[s] + [m_x1[b]], sg[s][:, :], x1_s[b, :, c, :], f"d_sg{s}")
                a = Q.put(AC, [l], lambda e, s=s: e.activation(sg[s][:, :], sg[s][:, :], ACT.Sigmoid), "a_z")
                t = Q.put(DV, [a, m], lambda e, s=s: e.tensor_tensor(sg[s][:, :], sg[s][:, :], rt[s][:, :], ALU.mult), "v_z")
                rt_free[s] = [t]
                h = Q.put(AC, [t] + bar, lambda e, c=c, s=s: e.activation(zh[b][:, c, :], sg[s][:, :], ACT.Copy), "a_z")
                l = Q.put(PL, [t, h] + bar, lambda e, c=c, s=s: e.tensor_tensor(
                    zl[b][:, c, :], sg[s][:, :], zh[b][:, c, :], ALU.subtract), "p_z")
                sg_free[s] = [l, h]
                z_ready[b] += [h, l]
                split_weights(1)

        a_min(0)
        b_min(0)
        a_exp(0)
        a_mul(0)
        b_exp(0)
        b_mul(0)
        e_exp(0)
        m_beta = early_constants()
        load_halves()
        work_until(0)
        split_weights(1)
        work_until(1)
        split_weights(1)
        work_until(2)
        split_weights(1)
        work_until(3)
        load_bet(0)
        for half in range(2):
            for part in range(2):
                vv(0, half, part)
        v_scaled(0)
        for which in "kq":
            for j in range(2):
                for part in range(2):
                    kq(0, which, j, part)
        split_weights(2)

        bg = 1250

        def fill(n, what):
            if n < len(order):
                if what[0] == "v":
                    vv(n, int(what[1]), int(what[2]))
                    if what == "v11":
                        D["vs_due"] = n
                else:
                    kq(n, what[0], int(what[1]), int(what[2]))
            split_weights(1)
            work(bg)

        for n in range(len(order)):
            nx = n + 1
            if nx < len(order):
                b = order[nx][1]
                if b not in y_ready or len(y_ready[b]) < 2 * NC:
                    work_until([i for i, t in enumerate(tiles) if t == (0, b, NC - 1)][0])
            burst = n % 4 == 0 and n > 0
            pieces = ["v00", "v01", "v10", "v11", "k00", "k01", "k10", "k11", "q00", "q01", "q10", "q11"]
            todo = [0]

            def between(k):
                if burst:
                    if todo[0] < 8:
                        wo(n - 1, todo[0])
                        todo[0] += 1
                        split_weights(1)
                        work(2 * bg)
                else:
                    for _ in range(k):
                        fill(nx, pieces[todo[0]])
                        todo[0] += 1

            s1(n)
            between(1)
            update(n, 0)
            between(1)
            recall(n, 1)
            between(2)
            turn_p(n)
            update(n, 1)
            between(1)
            recall(n, 2)
            pv(n)
            join(n, 0)
            if nx < len(order) and not burst:
                v_scaled(nx)
            between(2)
            update(n, 2)
            join(n, 1)
            between(1)
            join(n, 2)
            recall(n, 3)
            join(n, 3)
            if nx < len(order):
                load_bet(nx)
            between(2)
            if burst:
                while todo[0] < 8:
                    between(1)
            turn_att(n)
            if burst:
                for p in pieces:
                    fill(nx, p)
                    if p == "v11" and nx < len(order):
                        v_scaled(nx)
            else:
                between(2)
            whole[0] = True
            work(bg)
            whole[0] = False
            if n >= len(order) - 2:
                work_until(len(tiles))
                modulate(n - len(order) + 2)
        for i in range(8):
            split_weights(1)
            wo(len(order) - 1, i)
        split_weights(2)
        bar = list(Q.last.values())
        ffn = [(g, b) for g in range(NG) for b in range(NB)]
        m_x = {b: Q.dma(bar + [m_x1[b]], x[:, b, :, :], x1_s[b], f"d_xx{b}") for b in range(NB)}
        modulate(2)
        modulate(3)

        names = list(banks)
        bi = [0]

        def next_bank():
            bi[0] += 1
            return names[bi[0] % 8]

        sgi = [0]
        h_used = {0: bar, 1: bar}

        def up(n):
            g, b = ffn[n]
            last = n + 1 == len(ffn) or ffn[n + 1][0] != g
            marks = []
            for j in range(2):
                m = {}
                bk = {}
                for k in "13":
                    wi = windex[k, g]
                    slot = wi % NRING
                    bk[k] = next_bank()
                    terms = [((wh[slot][:, 256 * c + 128 * j:256 * c + 128 * j + 128],
                               wl[slot][:, 256 * c + 128 * j:256 * c + 128 * j + 128]),
                              (zh[b][:, c, :], zl[b][:, c, :])) for c in range(NC)]
                    m[k] = passes(bk[k], banks[bk[k]][:, :], terms, W["ready"][wi] + z_ready[b], "pe_g")
                    if last and j == 1:
                        W["used"][wi] = [m[k]]
                s = sgi[0] % 6
                sgi[0] += 1
                t_ = sg[s]
                g_, u_ = banks[bk["1"]], banks[bk["3"]]
                a = Q.put(AC, [m["1"]] + sg_free[s], lambda e, t_=t_, g_=g_: e.activation(t_[:, :], g_[:, :], ACT.Sigmoid), "a_f")
                t = Q.put(DV, [a], lambda e, t_=t_, g_=g_: e.tensor_tensor(t_[:, :], g_[:, :], t_[:, :], ALU.mult), "v_f")
                bank_free[bk["1"]] = [t]
                t = Q.put(DV, [t, m["3"]], lambda e, t_=t_, u_=u_: e.tensor_tensor(t_[:, :], u_[:, :], t_[:, :], ALU.mult), "v_f")
                bank_free[bk["3"]] = [t]
                o = n % 2
                h = Q.put(AC, [t] + h_used[o], lambda e, t_=t_, o=o, j=j: e.activation(hh[o][:, j, :], t_[:, :], ACT.Copy), "a_f")
                l = Q.put(PL, [h, t] + h_used[o], lambda e, t_=t_, o=o, j=j: e.tensor_tensor(
                    hl[o][:, j, :], t_[:, :], hh[o][:, j, :], ALU.subtract), "p_f")
                sg_free[s] = [l, h]
                marks += [h, l]
                split_weights(1)
            F[n] = marks

        def down(n):
            g, b = ffn[n]
            last = n + 1 == len(ffn) or ffn[n + 1][0] != g
            wi = windex["2", g]
            slot = wi % NRING
            o = n % 2
            for dc in range(NC):
                bank = next_bank()
                terms = [((wh[slot][:, 512 * j + 128 * dc:512 * j + 128 * dc + 128],
                           wl[slot][:, 512 * j + 128 * dc:512 * j + 128 * dc + 128]),
                          (hh[o][:, j, :], hl[o][:, j, :])) for j in range(2)]
                m = passes(bank, banks[bank][:, :], terms, W["ready"][wi] + F[n], "pe_g")
                a = Q.put(DV, [m, m_x[b]], lambda e, bank=bank, dc=dc: e.tensor_tensor(
                    x[:, b, dc, :], x[:, b, dc, :], banks[bank][:, :], ALU.add), "v_x")
                bank_free[bank] = [a]
                if g == NG - 1:
                    outs.append(Q.dma([a], out_d[b, :, dc, :], x[:, b, dc, :], "d_out"))
            h_used[o] = [m]
            if last:
                W["used"][wi] = [m]
                split_weights(2)

        outs = []
        for n in range(len(ffn) + 1):
            if n < len(ffn):
                up(n)
            if n > 0:
                down(n - 1)
        Q.put(SP, [outs[-1]], None)

        Q.run(ctx.enter_context(nc.Block()))


_OUT = (NB, P, NC, T)


def kernel(x, fside_BxSxS_0, cond_512, L0_cond_w, L0_cond_u, L0_attn_Wq, L0_attn_Wk, L0_attn_Wv, L0_attn_Wo,
           L0_attn_betas, L0_cond2_w, L0_cond2_u, L0_ffn_W1, L0_ffn_W2, L0_ffn_W3):
    import numpy as np
    import concourse.bacc as bacc
    from concourse.bass_utils import run_bass_kernel_spmd as run

    def fresh(a):
        return np.ascontiguousarray(a)

    def channels(a):
        a = np.asarray(a).reshape(NB, T, NC, P)
        return fresh(a.transpose(0, 3, 2, 1))

    def columns(w):
        a = np.asarray(w).reshape(NC, P, NG, 256)
        return fresh(a.transpose(2, 1, 0, 3)).reshape(NG, P, 2, 512)

    ident = np.eye(P, dtype=np.float32)
    mask = np.where(np.tril(np.ones((P, P), bool)), np.float32(0), np.float32(NEG)).astype(np.float32)
    had = np.ones((1, 1), np.float32)
    while had.shape[0] < P:
        had = np.block([[had, had], [had, -had]]).astype(np.float32)
    wo = fresh(np.asarray(L0_attn_Wo).reshape(NG, 2, P, C).transpose(0, 2, 1, 3))
    w2 = np.asarray(L0_ffn_W2).T.reshape(16, P, 8, 64)
    wu = np.stack([np.asarray(a).reshape(NC, P).T for a in (L0_cond_w, L0_cond_u, L0_cond2_w, L0_cond2_u)], 1)
    arrays = {
        "xT": channels(x), "fT": channels(fside_BxSxS_0),
        "cond": fresh(np.asarray(cond_512).reshape(1, NB * P)), "wu": fresh(wu),
        "wq": columns(L0_attn_Wq), "wk": columns(L0_attn_Wk), "wv": columns(L0_attn_Wv),
        "wo": wo, "betas": fresh(np.asarray(L0_attn_betas).reshape(H, P)),
        "w1": columns(np.asarray(L0_ffn_W1).T), "w3": columns(np.asarray(L0_ffn_W3).T),
        "w2": fresh(w2.transpose(2, 1, 0, 3)), "ident": ident, "mask": mask, "had": had,
    }
    nc = bacc.Bacc("TRN2", target_bir_lowering=False, num_devices=1)
    args = [nc.dram_tensor("in_" + k, list(a.shape), F32, kind="ExternalInput").ap() for k, a in arrays.items()]
    args.append(nc.dram_tensor("out_0", list(_OUT), F32, kind="ExternalOutput").ap())
    adaln_attn_ffn(nc, *args)
    r = run(nc, [{"in_" + k: a for k, a in arrays.items()}], core_ids=[0])
    got = np.asarray(r.results[0]["out_0"])
    return np.ascontiguousarray(got.transpose(0, 3, 2, 1)).reshape(NB, T, C)
```

```python
from contextlib import ExitStack

import concourse.bass as bass
from concourse import mybir

F32 = mybir.dt.float32
F32R = mybir.dt.float32r
ALU = mybir.AluOpType
ACT = mybir.ActivationFunctionType
AX_X = mybir.AxisListType.X

P = 128
NB = 4
T = 512
C = 512
NC = C // P
H = 16
SEG = 128
NSEG = T // SEG
NG = 8
NRING = 6
NSTAGE = 4
BG = 750
A = 800
STEADY = [0, A, A, 0, A, A, 0, A, A, A, A, A]
BURST = [A] * 8
AFTER = 1200
LATE = 1200
HID = 2048
SCALE = float(P) ** -0.5
RSQ = float(HID) ** -0.5
NEG = -3.0e38
PE, DV, AC, PL, SP = "tensor", "vector", "scalar", "gpsimd", "sync"


class Queues:

    def __init__(self, nc, ctx):
        self.nc, self.ctx = nc, ctx
        self.todo = {e: [] for e in (PE, DV, AC, PL, SP)}
        self.sems, self.count, self.seen = {}, {}, {}
        self.last = {}

    def step(self, name, by):
        if name not in self.sems:
            self.sems[name] = self.ctx.enter_context(self.nc.semaphore(name))
            self.count[name] = 0
        self.count[name] += by
        return name, self.count[name]

    def put(self, eng, waits, fn, name=None, by=1):
        need = []
        for n, v in waits:
            if self.seen.get((eng, n), 0) < v:
                self.seen[(eng, n)] = v
                need = [x for x in need if x[0] != n] + [(n, v)]
        mark = self.step(name, by) if name else None
        if mark:
            self.last[(eng, name)] = mark
        self.todo[eng].append((need, fn, name, by))
        return mark

    def dma(self, waits, out, in_, name):
        return self.put(SP, waits, lambda e: e.dma_start(out, in_), name, 16)

    def run(self, block):
        def program(todo):
            def body(e):
                for need, fn, name, by in todo:
                    for n, v in need:
                        e.wait_ge(self.sems[n], v)
                    if fn is None:
                        continue
                    ins = fn(e)
                    if name:
                        ins.then_inc(self.sems[name], by)
            return body
        block.tensor(program(self.todo[PE]))
        block.vector(program(self.todo[DV]))
        block.scalar(program(self.todo[AC]))
        block.gpsimd(program(self.todo[PL]))
        block.sync(program(self.todo[SP]))


def adaln_attn_ffn(nc, xT_d, fT_d, cond_d, wu_d, wq_d, wk_d, wv_d, wo_d, betas_d,
                   w1_d, w3_d, w2_d, ident_d, mask_d, had_d, out_d):
    beta_s = nc.dram_tensor("beta_s", [2, H, P], F32).ap()
    ratio_s = nc.dram_tensor("ratio_s", [NB, NC, P, T], F32).ap()
    x1_s = nc.dram_tensor("x1_s", [NB, P, NC, T], F32).ap()
    w2_s = nc.dram_tensor("w2_s", [8, P, 16, 64], F32).ap()

    with ExitStack() as ctx:
        Q = Queues(nc, ctx)

        def sb(stack, name, shape, dt=F32):
            return stack.enter_context(nc.sbuf_tensor(name, shape, dt))

        banks = {n: ctx.enter_context(nc.psum_tensor("ps" + n, [P, 512], F32))
                 for n in ("G0", "G1", "X0", "X1", "Y0", "Y1", "Z0", "Z1")}

        yh = [sb(ctx, f"yh{i}", [P, NC, T], F32R) for i in range(2)]
        yl = [sb(ctx, f"yl{i}", [P, NC, T], F32R) for i in range(2)]
        wh = [sb(ctx, f"wh{i}", [P, 1024], F32R) for i in range(NRING)]
        wl = [sb(ctx, f"wl{i}", [P, 1024], F32R) for i in range(NRING)]
        stage = [sb(ctx, f"stage{i}", [P, 512]) for i in range(NSTAGE)]
        wu = sb(ctx, "wu", [P, 4, NC])
        ucut = sb(ctx, "ucut", [P, 2, NC])
        dec0 = sb(ctx, "dec0", [P, 2, NC])
        dec = sb(ctx, "dec", [P, NB, 2, NC])
        tf = sb(ctx, "tf", [P, 4, NB])

        two = ExitStack()
        kx = [sb(two, f"kx{i}", [P, T]) for i in range(2)]
        EK, EKV, EU, EUV, NF, DF, ER, OY = (
            sb(two, n, [P, T]) for n in ("EK", "EKV", "EU", "EUV", "NF", "DF", "ER", "OY"))
        NBK = sb(two, "NBK", [P, T + 1])
        DBK = sb(two, "DBK", [P, T + 1])
        two.close()
        three = ExitStack()
        HA, HB, HO = (sb(three, n, [P, 1024]) for n in ("HA", "HB", "HO"))
        HH = sb(three, "HH", [P, 1024], F32R)
        HL = sb(three, "HL", [P, 1024], F32R)
        hadf = sb(three, "hadf", [P, P])
        had = sb(three, "had", [P, P], F32R)
        three.close()
        sg = [sb(ctx, f"sg{i}", [P, T]) for i in range(6)]
        rt = [sb(ctx, f"rt{i}", [P, T]) for i in range(2)]
        hh = [sb(ctx, "hh0", [P, 2, T], F32R)]
        hl = [sb(ctx, "hl0", [P, 2, T], F32R)]
        sb(ctx, "pad", [P, 32])

        one = ExitStack()
        xb = sb(one, "xb", [P, NC, T])
        ah = sb(one, "ah", [P, 16, 256], F32R)
        al = sb(one, "al", [P, 16, 256], F32R)
        qT = sb(one, "qT", [P, 2, T])
        kT = sb(one, "kT", [P, 2, T])
        sq = sb(one, "sq", [P, 2, T])
        sk = sb(one, "sk", [P, 2, T])
        v = [sb(one, f"v{i}", [P, NSEG, 2, P + 1]) for i in range(2)]
        vs = sb(one, "vs", [P, NSEG, 2, P])
        S = sb(one, "S", [P, 2, T])
        pT = sb(one, "pT", [P, 2, T])
        kn = sb(one, "kn", [P, 2, 3, P])
        t2 = sb(one, "t2", [P, 2, 3, P])
        mem = sb(one, "mem", [P, 2, P + 1])
        mem0 = sb(one, "mem0", [P, P + 1])
        delta = sb(one, "delta", [P, 2, P + 1])
        bet = sb(one, "bet", [P, 256])
        omb = sb(one, "omb", [P, 256])
        etmps = [sb(one, f"etmp{i}", [P, T]) for i in range(2)]
        ident = sb(one, "ident", [P, P])
        mask = sb(one, "mask", [P, P])
        st = sb(one, "st", [P, 4, 2, NSEG])
        rz = sb(one, "rz", [P, 2, 2])
        one.close()
        x = sb(ctx, "x", [P, NB, NC, T])
        zh = yh + [sb(ctx, f"zh{i}", [P, NC, T], F32R) for i in (2, 3)]
        zl = yl + [sb(ctx, f"zl{i}", [P, NC, T], F32R) for i in (2, 3)]
        hh += [sb(ctx, "hh1", [P, 2, T], F32R)]
        hl += [sb(ctx, "hl1", [P, 2, T], F32R)]

        cb = S[:, 0, :]
        bt = S[0:H, 1, 0:P]
        m_wu = Q.dma([], wu[:, :, :], wu_d, "d_wu")
        m_cb = Q.dma([], cb, cond_d.to_broadcast([P, NB * P]), "d_cb")
        m_kx = {}
        for i in range(2):
            m_kx[i] = Q.dma([], kx[i][:, :], fT_d[0, :, i, :], f"d_k{i}")
        m_er = {0: Q.dma([], ER[:, :], xT_d[0, :, 0, :], "d_er")}
        m_xb = {0: Q.dma([], xb[:, :, :], xT_d[0], "d_xb")}
        m_bt = Q.dma([], bt, betas_d, "d_bt")
        m_id = Q.dma([], ident[:, :], ident_d, "d_id")
        m_mk = Q.dma([], mask[:, :], mask_d, "d_mk")

        e_w = Q.put(AC, [m_wu], lambda e: e.activation(dec0[:, :, :], wu[:, 0:4:2, :], ACT.Exp), "a_c")
        e_w = Q.put(AC, [e_w], lambda e: e.activation(dec0[:, :, :], dec0[:, :, :], ACT.Exp, scale=-1.0), "a_c")
        c1 = Q.put(DV, [m_cb], lambda e: e.tensor_reduce(
            tf[:, 0, :], cb.rearrange("p (b t) -> p b t", b=NB), AX_X, ALU.add), "v_c")
        e_t = Q.put(AC, [c1], lambda e: e.activation(tf[:, 1, :], tf[:, 0, :], ACT.Exp, scale=-1.0), "a_c")
        c1 = Q.put(DV, [e_t], lambda e: e.tensor_scalar_add(tf[:, 1, :], tf[:, 1, :], 1.0), "v_c")
        c1 = Q.put(DV, [c1], lambda e: e.reciprocal(tf[:, 0, :], tf[:, 1, :]), "v_c")
        c1 = Q.put(DV, [c1], lambda e: e.tensor_scalar(tf[:, 1, :], tf[:, 0, :], 0.5, 0.5, ALU.mult, ALU.add), "v_c")
        m_s = Q.put(DV, [c1], lambda e: e.tensor_scalar(tf[:, 2, :], tf[:, 0, :], 0.2, 0.8, ALU.mult, ALU.add), "v_c")
        for b in range(NB):
            m_dec = Q.put(DV, [c1, m_s, e_w], lambda e, b=b: e.tensor_scalar(
                dec[:, b, :, :], dec0[:, :, :], tf[:, 1, b:b + 1], None, ALU.mult), "v_c")
        m_cut = Q.put(DV, [m_wu], lambda e: e.tensor_scalar(
            ucut[:, :, :], wu[:, 1:4:2, :], -1.0, 30.0, ALU.mult, ALU.add), "v_c")
        m_nb0 = Q.put(DV, [], lambda e: e.memset(NBK[:, T:T + 1], 0.0), "v_c")
        m_nb0 = Q.put(DV, [], lambda e: e.memset(DBK[:, T:T + 1], 0.0), "v_c")

        def early_constants():
            e_b = Q.put(AC, [m_bt], lambda e: e.activation(bt, bt, ACT.Exp, scale=-1.0), "a_c")
            c = Q.put(DV, [e_b], lambda e: e.tensor_scalar_add(bt, bt, 1.0), "v_c")
            c = Q.put(DV, [c], lambda e: e.reciprocal(S[0:H, 1, P:2 * P], bt), "v_c")
            c = Q.put(DV, [c], lambda e: e.tensor_scalar(
                S[0:H, 1, 2 * P:3 * P], S[0:H, 1, P:2 * P], -1.0, 1.0, ALU.mult, ALU.add), "v_c")
            a = Q.dma([c], beta_s[0], S[0:H, 1, P:2 * P], "d_b0")
            b = Q.dma([c], beta_s[1], S[0:H, 1, 2 * P:3 * P], "d_b1")
            for t in v:
                Q.put(DV, [], lambda e, t=t: e.memset(t[:, :, :, P:P + 1], 1.0), "v_c")
            Q.put(DV, [], lambda e: e.memset(mem0[:, 0:P], 0.0), "v_c")
            Q.put(DV, [], lambda e: e.memset(mem0[:, P:P + 1], 1.0 / P), "v_c")
            d = Q.put(DV, [], lambda e: e.memset(delta[:, :, P:P + 1], 1.0), "v_c")
            return a, b, d

        order = [(g, b) for b in range(NB) for g in range(NG)]
        stream, windex = [], {}

        def streamed(k, g, key):
            windex[k, key] = len(stream)
            stream.append((k, g))

        for n in range(-1, len(order)):
            if n >= 0 and n % 4 == 0 and n > 0:
                for i in range(8):
                    streamed("o", i, (n - 1, i))
            if n + 1 < len(order):
                for k in "vkq":
                    streamed(k, order[n + 1][0], n + 1)
        streamed("1", 0, 0)
        streamed("3", 0, 0)
        for i in range(8):
            streamed("o", i, (len(order) - 1, i))
        streamed("2", 0, 0)
        for g in range(1, NG):
            for k in "132":
                streamed(k, g, g)
        src = {"q": wq_d, "k": wk_d, "v": wv_d, "o": wo_d, "1": w1_d, "3": w3_d}
        W = {"next": 0, "load": 0, "split": 0, "half": [], "ready": {}, "slot": {},
             "free": [(i, []) for i in range(NRING)]}
        stage_free = [[] for _ in range(NSTAGE)]
        m_w2s = []

        def load_halves():
            while W["load"] < 2 * len(stream) and W["load"] < W["split"] + NSTAGE:
                i, half = divmod(W["load"], 2)
                k, g = stream[i]
                if k == "2" and not m_w2s:
                    return
                s = W["load"] % NSTAGE
                if k == "2":
                    out = stage[s][:, :].rearrange("p (n a d) -> p n a d", n=4, a=2)
                    in_ = w2_s[4 * half:4 * half + 4, :, 2 * g:2 * g + 2, :].rearrange("n p a d -> p n a d")
                    m = Q.dma(stage_free[s] + m_w2s, out, in_, f"d_w{s}")
                else:
                    m = Q.dma(stage_free[s], stage[s][:, :], src[k][g, :, half, :], f"d_w{s}")
                W["half"].append(m)
                W["load"] += 1

        def split_weights(limit=1):
            n = 0
            while W["next"] < len(stream) and n < limit:
                i = W["next"]
                k = stream[i][0]
                if not W["free"]:
                    return
                load_halves()
                if W["load"] < 2 * i + 2 and k == "2" and not m_w2s:
                    return
                slot, free = W["free"].pop(0)
                W["slot"][i] = slot
                marks = []
                for half in range(2):
                    s = (2 * i + half) % NSTAGE
                    m_in = W["half"][2 * i + half]
                    if k == "2":
                        hi = wh[slot][:, :].rearrange("p (a n d) -> p n a d", a=2, n=8)[:, 4 * half:4 * half + 4]
                        lo = wl[slot][:, :].rearrange("p (a n d) -> p n a d", a=2, n=8)[:, 4 * half:4 * half + 4]
                        raw = stage[s][:, :].rearrange("p (n a d) -> p n a d", n=4, a=2)
                    else:
                        hi = wh[slot][:, 512 * half:512 * half + 512]
                        lo = wl[slot][:, 512 * half:512 * half + 512]
                        raw = stage[s][:, :]
                    if k == "o":
                        a = Q.put(AC, [m_in] + free, lambda e, hi=hi, raw=raw: e.activation(hi, raw, ACT.Copy), "a_wh")
                    else:
                        a = Q.put(PL, [m_in] + free, lambda e, hi=hi, raw=raw: e.tensor_scalar(
                            hi, raw, 1.0, 0.0, ALU.mult, ALU.add), "p_wh")
                    p = Q.put(PL, [a, m_in] + free, lambda e, lo=lo, raw=raw, hi=hi: e.tensor_tensor(
                        lo, raw, hi, ALU.subtract), "p_wl")
                    stage_free[s] = [a, p]
                    marks += [a, p]
                    W["split"] += 1
                    load_halves()
                    if half == 0 and W["load"] < 2 * i + 2:
                        raise AssertionError("a weight's second half is not there")
                W["next"] = i + 1
                W["ready"][i] = marks
                n += 1

        bank_free = {n: [] for n in banks}

        def passes(bank, out, terms, waits, name, part=(0, 1), free=True):
            k, n = part
            if free and k == 0:
                waits = waits + bank_free[bank]
            pairs = [p for (lh, ll), (rh, rl) in terms for p in ((lh, rh), (lh, rl), (ll, rh))]
            first, end = k * len(pairs) // n, (k + 1) * len(pairs) // n
            for i in range(first, end):
                a, c = pairs[i]
                m = Q.put(PE, waits if i == first else [], lambda e, a=a, c=c, i=i: e.matmul(
                    out, a, c, start=(i == 0), stop=(i == len(pairs) - 1)), name if i == len(pairs) - 1 else None)
            return m

        y_ready = {}
        y_free = {0: [], 1: []}
        tiles = [(i, b, c) for i, b in ((0, 0), (0, 1), (1, 0), (0, 2), (1, 1), (0, 3), (1, 2), (1, 3)) for c in range(NC)]
        B = {"EK": [], "EU": [], "N": [], "kfree": {0: [], 1: []}, "ER": [], "OY": []}
        m_ratio = {}
        A = {n: {} for n in range(len(tiles) + 1)}
        firsts = [n for n, t in enumerate(tiles) if t[0] == 0]

        def k_load(n):
            if 2 <= n < len(tiles):
                _, b, c = tiles[n]
                m_kx[n] = Q.dma(B["kfree"][n % 2], kx[n % 2][:, :], fT_d[b, :, c, :], f"d_k{n % 2}")

        def er_load(n):
            if n in firsts and n > 0:
                _, b, c = tiles[n]
                m_er[n] = Q.dma(B["ER"], ER[:, :], xT_d[b, :, c, :], "d_er")

        def a_min(n):
            if n < len(tiles):
                k = kx[n % 2][:, :]
                A[n]["mn"] = Q.put(DV, [m_kx[n]] + B["EK"], lambda e: e.tensor_scalar(EK[:, :], k, 30.0, None, ALU.min), "v_sc")

        def a_exp(n):
            if n < len(tiles):
                A[n]["ek"] = Q.put(AC, [A[n]["mn"]], lambda e: e.activation(EK[:, :], EK[:, :], ACT.Exp), "a_ek")

        def a_mul(n):
            if n < len(tiles):
                k = kx[n % 2][:, :]
                A[n]["ekv"] = Q.put(PL, [A[n]["ek"]] + B["EK"], lambda e: e.tensor_tensor(EKV[:, :], EK[:, :], k, ALU.mult), "p_ekv")

        def b_min(n):
            if n < len(tiles):
                k, (i, b, c) = kx[n % 2][:, :], tiles[n]
                A[n]["mu"] = Q.put(DV, [m_kx[n], m_cut] + B["EU"], lambda e: e.tensor_scalar(
                    EU[:, :], k, ucut[:, i, c:c + 1], None, ALU.min), "v_sc")

        def b_exp(n):
            if n < len(tiles):
                i, b, c = tiles[n]
                A[n]["eu"] = Q.put(AC, [A[n]["mu"]], lambda e: e.activation(
                    EU[:, :], EU[:, :], ACT.Exp, bias=wu[:, 2 * i + 1, c:c + 1]), "a_eu")

        def b_mul(n):
            if n < len(tiles):
                k = kx[n % 2][:, :]
                A[n]["euv"] = Q.put(PL, [A[n]["eu"]] + B["EU"], lambda e: e.tensor_tensor(EUV[:, :], EU[:, :], k, ALU.mult), "p_euv")
                B["kfree"][n % 2] = [A[n]["euv"], A[n]["ekv"]]

        def e_exp(n):
            if n in firsts:
                A[n]["er"] = Q.put(AC, [m_er[n]], lambda e: e.activation(ER[:, :], ER[:, :], ACT.Exp, scale=-1.0), "a_er")

        def scan_steps(n):
            i, b, c = tiles[n]
            d = dec[:, b, i, c:c + 1]
            db = d.to_broadcast([P, T])
            M = {}
            after = ([f for f in firsts if f > n] or [None])[0]

            def s1():
                k_load(n + 2)
                M["nf"] = Q.put(DV, [A[n]["ekv"], m_dec] + B["N"], lambda e: e.tensor_tensor_scan(
                    NF[:, :], db, EKV[:, :], 0.0, ALU.mult, ALU.add), "v_sc")

            def s2():
                M["nb"] = Q.put(DV, [A[n]["ekv"]], lambda e: e.tensor_tensor_scan(
                    NBK[:, T - 1::-1], db, EKV[:, ::-1], 0.0, ALU.mult, ALU.add), "v_sc")

            def s3():
                M["df"] = Q.put(DV, [A[n]["ek"]], lambda e: e.tensor_tensor_scan(
                    DF[:, :], db, EK[:, :], 0.0, ALU.mult, ALU.add), "v_sc")

            def s4():
                M["db"] = Q.put(DV, [A[n]["ek"]], lambda e: e.tensor_tensor_scan(
                    DBK[:, T - 1::-1], db, EK[:, ::-1], 0.0, ALU.mult, ALU.add), "v_sc")
                B["EK"] = [M["db"]]

            def n1():
                M["n"] = Q.put(DV, [M["nb"], m_nb0], lambda e: e.scalar_tensor_tensor(
                    NF[:, :], NBK[:, 1:T + 1], d, NF[:, :], ALU.mult, ALU.add), "v_sc")

            def n2():
                M["n"] = Q.put(DV, [M["n"], A[n]["euv"]], lambda e: e.tensor_tensor(
                    NF[:, :], NF[:, :], EUV[:, :], ALU.add), "v_sc")

            def d1():
                M["d"] = Q.put(DV, [M["db"]], lambda e: e.scalar_tensor_tensor(
                    DF[:, :], DBK[:, 1:T + 1], d, DF[:, :], ALU.mult, ALU.add), "v_sc")

            def d2():
                M["d"] = Q.put(DV, [M["d"], A[n]["eu"]], lambda e: e.tensor_tensor(
                    DF[:, :], DF[:, :], EU[:, :], ALU.add), "v_sc")
                B["EU"] = [M["d"]]

            def d3():
                M["d"] = Q.put(DV, [M["d"]], lambda e: e.tensor_scalar(
                    DF[:, :], DF[:, :], 1e-8, None, ALU.max), "v_sc")

            def d4():
                if i == 0:
                    M["d"] = Q.put(DV, [M["d"], A[n]["er"]], lambda e: e.scalar_tensor_tensor(
                        DF[:, :], ER[:, :], 1.0, DF[:, :], ALU.add, ALU.mult), "v_sc")
                    B["ER"] = [M["d"]]

            def rc(j):
                M["r"] = Q.put(DV, [M["d"]], lambda e: e.reciprocal(
                    DBK[:, 128 * j:128 * j + 128], DF[:, 128 * j:128 * j + 128]), "v_sc")
                if j == 0 and i == 0 and after is not None:
                    er_load(after)

            def out():
                M["o"] = Q.put(DV, [M["r"]] + B["OY"], lambda e: e.scalar_tensor_tensor(
                    OY[:, :], NF[:, :], tf[:, 2, b:b + 1], DBK[:, 0:T], ALU.mult, ALU.mult), "v_sc")
                B["N"] = [M["o"]]

            def store():
                m = M["o"]
                if i == 0:
                    s = b % 2
                    free = y_free.get(b, [])
                    h = Q.put(AC, [m] + free, lambda e: e.activation(yh[s][:, c, :], OY[:, :], ACT.Copy), "a_yh")
                    l = Q.put(PL, [h, m] + free, lambda e: e.tensor_tensor(
                        yl[s][:, c, :], OY[:, :], yh[s][:, c, :], ALU.subtract), "p_yl")
                    y_ready.setdefault(b, []).extend([h, l])
                    B["OY"] = [l, h]
                else:
                    s = Q.dma([m], ratio_s[b, c], OY[:, :], "d_rs")
                    m_ratio[b, c] = s
                    B["OY"] = [s]

            N = n + 1
            return [(600, s1), (600, s2), (600, s3), (600, s4), (0, lambda: e_exp(n) if n > 0 else None), (335, lambda: a_min(N)), (660, n1), (600, n2),
                    (0, lambda: a_exp(N)), (660, d1), (600, d2), (335, lambda: b_min(N)), (0, lambda: a_mul(N)),
                    (335, d3), (660 if i == 0 else 0, d4), (0, lambda: b_exp(N)), (880, lambda: rc(0)),
                    (880, lambda: rc(1)), (0, lambda: b_mul(N)), (880, lambda: rc(2)), (880, lambda: rc(3)),
                    (700, out), (0, store)]

        def had_steps():
            M = {}

            def first():
                bar = [Q.last[DV, "v_sc"], Q.last[PL, "p_ekv"], Q.last[PL, "p_euv"], Q.last[AC, "a_eu"],
                       Q.last[AC, "a_ek"], Q.last[AC, "a_yh"], Q.last[AC, "a_er"], Q.last[SP, "d_rs"],
                       Q.last[PL, "p_yl"]]
                M["ha"] = bar
                M["out"] = bar
                M["hb"] = bar
                d = Q.dma(bar, hadf[:, :], had_d, "d_had")
                M["had"] = Q.put(AC, [d], lambda e: e.activation(had[:, :], hadf[:, :], ACT.Copy), "a_had")
                M["load"] = Q.dma(bar, HA[:, :], w2_d[0].rearrange("p a d -> p (a d)"), "d_h")

            def level(lv):
                w = 64 << lv
                a = [HA, HB][lv % 2][:, :].rearrange("p (x t w) -> p x t w", t=2, w=w)
                o = [HB, HA][lv % 2][:, :].rearrange("p (x t w) -> p x t w", t=2, w=w)
                waits = [M["load"]] if lv == 0 else [M["lv"]]
                if lv == 0:
                    waits = waits + M["hb"]
                Q.put(DV, waits, lambda e: e.tensor_tensor(
                    o[:, :, 0, :], a[:, :, 0, :], a[:, :, 1, :], ALU.add), "v_h")
                M["lv"] = Q.put(DV, [], lambda e: e.tensor_tensor(
                    o[:, :, 1, :], a[:, :, 0, :], a[:, :, 1, :], ALU.subtract), "v_h")

            def parts(n):
                M["hi"] = Q.put(AC, [M["lv"]] + M.get("pe", M["ha"]), lambda e: e.activation(HH[:, :], HA[:, :], ACT.Copy), "a_h")

            def low():
                M["lo"] = Q.put(DV, [M["hi"]] + M.get("pe", M["ha"]), lambda e: e.tensor_tensor(
                    HL[:, :], HA[:, :], HH[:, :], ALU.subtract), "v_h")
                M["hb"] = [M["lo"]]

            def load(n):
                M["load"] = Q.dma([M["lo"], M["hi"]], HA[:, :], w2_d[n + 1].rearrange("p a d -> p (a d)"), "d_h")

            def mult(n, j):
                bank = next_g()
                bk = banks[bank]
                cut = slice(512 * j, 512 * j + 512)
                Q.put(PE, bank_free[bank] + [M["had"], M["hi"], M["lo"]], lambda e: e.matmul(
                    bk[:, :], had[:, :], HH[:, cut], start=True, stop=False))
                m = Q.put(PE, [], lambda e: e.matmul(
                    bk[:, :], had[:, :], HL[:, cut], start=False, stop=True), "pe_h")
                M["pe"] = [m]
                o = Q.put(AC, [m] + M["out"], lambda e: e.activation(
                    HO[:, cut], bk[:, :], ACT.Copy, scale=RSQ), "a_ho")
                bank_free[bank] = [o]
                M["ho"] = o

            def save(n):
                M["out"] = [Q.dma([M["ho"]], w2_s[n].rearrange("p a d -> p (a d)"), HO[:, :], "d_ho")]
                if n == 7:
                    m_w2s[:] = M["out"]

            steps = [(1000, first)]
            for n in range(8):
                steps += [(1250, lambda lv=lv: level(lv)) for lv in range(4)]
                steps += [(1000, lambda n=n: parts(n)), (1000, wait), (1250, low), (1000, wait)]
                if n < 7:
                    steps += [(0, lambda n=n: load(n))]
                steps += [(0, None), (1000, lambda n=n: mult(n, 0)), (0, None), (1000, lambda n=n: mult(n, 1)),
                          (1000, wait), (0, lambda n=n: save(n))]
            return steps

        def wait():
            return

        gi = [0]

        def next_g():
            gi[0] += 1
            return f"G{gi[0] % 2}"

        background = []
        for n in range(len(tiles)):
            background += [(cost, fn, n) for cost, fn in scan_steps(n)]
        background += [(cost, fn, len(tiles)) for cost, fn in had_steps()]
        at = [0]
        whole = [False]

        def work(ns):
            while ns > 0 and at[0] < len(background):
                cost, fn, tile = background[at[0]]
                if tile < len(tiles) and tiles[tile][0] == 0 and tiles[tile][1] not in y_free:
                    return
                if tile > len(tiles) and tile - len(tiles) + 3 not in y_free:
                    return
                if fn is None and not whole[0]:
                    return
                at[0] += 1
                if fn is not None:
                    fn()
                ns -= cost

        def work_until(tile):
            while at[0] < len(background) and background[at[0]][2] <= tile:
                fn = background[at[0]][1]
                at[0] += 1
                if fn is not None:
                    fn()

        D = {}
        behind, before = [], []

        def kq(n, which, j, part):
            g, b = order[n]
            wi = windex[which, n]
            slot, ys = W["slot"][wi], b % 2
            if part == 0:
                D["bank"] = next_g()
            bank = D["bank"]
            terms = [((wh[slot][:, 256 * c + 128 * j:256 * c + 128 * j + 128],
                       wl[slot][:, 256 * c + 128 * j:256 * c + 128 * j + 128]),
                      (yh[ys][:, c, :], yl[ys][:, c, :])) for c in range(NC)]
            assert len(y_ready[b]) == 2 * NC
            m = passes(bank, banks[bank][:, :], terms, W["ready"][wi] + y_ready[b], "pe_g", part=(part, 2))
            if part == 0:
                return
            if j == 1:
                W["free"].append((slot, [m]))
                if g == NG - 1 and which == "q":
                    y_free[b + 2] = [m]
            dst, sig = (qT, sq) if which == "q" else (kT, sk)
            a = Q.put(AC, [m] + D.get("scores", []), lambda e: e.activation(dst[:, j, :], banks[bank][:, :], ACT.Copy), "a_qk")
            bank_free[bank] = [a]
            D[which, j] = a
            etmp = etmps[j]
            p = Q.put(AC, [m] + D.get(("etmp", j), []), lambda e: e.activation(
                etmp[:, :], banks[bank][:, :], ACT.Relu, scale=-1.0), "a_mn")
            bank_free[bank] = [p]
            x2 = Q.put(AC, [p], lambda e: e.activation(etmp[:, :], etmp[:, :], ACT.Exp, scale=-1.0), "a_e")

            def sigma():
                old = D.get("am3" if which == "q" else "dk2", [])
                s = Q.put(DV, [x2, a] + old, lambda e: e.scalar_tensor_tensor(
                    sig[:, j, :], dst[:, j, :], 1.0, etmp[:, :], ALU.add, ALU.max), "v_sg")
                D["etmp", j] = [s]
                D["s" + which, j] = s

            behind.append(sigma)

        def vv(n, half, part):
            g, b = order[n]
            wi = windex["v", n]
            slot, ys = W["slot"][wi], b % 2
            if part == 0:
                D["bank"] = next_g()
            bank = D["bank"]
            bk = banks[bank]
            t = 2 * half + part
            terms = [((yh[ys][:, c, 128 * t:128 * t + 128], yl[ys][:, c, 128 * t:128 * t + 128]),
                      (wh[slot][:, 256 * c:256 * c + 256], wl[slot][:, 256 * c:256 * c + 256])) for c in range(NC)]
            m = passes(bank, bk[:, 256 * part:256 * part + 256], terms, W["ready"][wi] + y_ready[b], "pe_g", free=(part == 0))
            if part == 0:
                return
            if half == 1:
                W["free"].append((slot, [m]))
            vt = v[n % 2]
            a = Q.put(AC, [m] + D.get(("u2", n - 2), []), lambda e: e.activation(
                vt[:, 2 * half:2 * half + 2, :, 0:P], bk[:, :].rearrange("p (t h d) -> p t h d", t=2, h=2), ACT.Copy), "a_v")
            bank_free[bank] = [a]
            D["v", n, half] = a

        def v_scaled(n):
            load_omb(n)
            vt = v[n % 2]
            for j in range(2):
                m = Q.put(PL, [D["v", n, 0], D["v", n, 1], D["omb"]] + D.get("pv", []), lambda e, j=j: e.tensor_tensor(
                    vs[:, :, j, :], vt[:, :, j, 0:P],
                    omb[:, 128 * j:128 * j + 128].rearrange("p (a d) -> p a d", a=1).to_broadcast([P, NSEG, P]),
                    ALU.mult), "p_vs")
            D["vs"] = m

        def load_omb(n):
            g = order[n][0]
            if True:
                w = [D["vs"]] if "vs" in D else []
                D["omb"] = Q.dma(w + [m_beta[1]], omb[:, :],
                                 beta_s[1, 2 * g:2 * g + 2, :].rearrange("(o h) d -> o (h d)", o=1).to_broadcast([P, 256]), "d_om")

        def load_bet(n):
            g = order[n][0]
            if True:
                w = D.get("t2_3", [])
                D["bet"] = Q.dma(w + [m_beta[0]], bet[:, :],
                                 beta_s[0, 2 * g:2 * g + 2, :].rearrange("(o h) d -> o (h d)", o=1).to_broadcast([P, 256]), "d_be")

        def wo(n, i):
            wi = windex["o", (n, i)]
            slot = W["slot"][wi]
            if i == 0:
                D["wo_banks"] = [next_g(), next_g()]
            for dc in range(NC):
                bank = D["wo_banks"][dc // 2]
                out = banks[bank][:, 256 * (dc % 2):256 * (dc % 2) + 256]
                pairs = []
                for jj in range(2):
                    lo = 512 * jj + 128 * dc
                    j = 2 * i + jj
                    pairs += [(wh[slot][:, lo:lo + 128], ah[:, j, :]), (wh[slot][:, lo:lo + 128], al[:, j, :]),
                              (wl[slot][:, lo:lo + 128], ah[:, j, :])]
                for k, (a, c) in enumerate(pairs):
                    start = i == 0 and k == 0 and dc % 2 == 0
                    stop = i == 7 and k == 5
                    w = (W["ready"][wi] + D["att"] + bank_free[bank]) if k == 0 else []
                    m = Q.put(PE, w, lambda e, a=a, c=c, out=out, start=start, stop=stop: e.matmul(
                        out, a, c, start=start, stop=stop, skip_group_check=True), "pe_o" if k == 5 else None)
                if i == 7 and dc % 2 == 1:
                    D["wo_done", dc // 2] = m
            W["free"].append((slot, [m]))
            if i < 7:
                return
            D["wo"] = [m]
            b, half = order[n][1], (n % 8) // 4
            for dc in range(NC):
                bank = D["wo_banks"][dc // 2]
                src_ = banks[bank][:, 256 * (dc % 2):256 * (dc % 2) + 256].rearrange("p (h s r) -> p h s r", h=8, s=4)
                dst = xb[:, dc, :].rearrange("p (s h r) -> p h s r", s=4, h=16)[:, 8 * half:8 * half + 8]
                a = Q.put(DV, [D["wo_done", dc // 2], m_xb[b]], lambda e, src_=src_, dst=dst: e.tensor_tensor(
                    dst, dst, src_, ALU.add), "v_x")
                bank_free[bank] = [a]
            if half == 1:
                def keep(dc):
                    m_x1[b] = Q.dma([a], x1_s[b, :, dc, :], xb[:, dc, :], "d_x1")

                def fetch(dc):
                    m_xb[b + 1] = Q.dma([m_x1[b]], xb[:, dc, :], xT_d[b + 1, :, dc, :], "d_xb")

                later.extend(lambda dc=dc: keep(dc) for dc in range(NC))
                if b + 1 < NB:
                    later.extend(lambda dc=dc: fetch(dc) for dc in range(NC))
                else:
                    while later:
                        later.pop(0)()

        m_x1 = {}
        later = []

        def seg(s):
            return slice(SEG * s, SEG * s + SEG)

        def s1(n):
            for j in range(2):
                bk = banks[f"Y{j}"]
                for s in range(3):
                    m = Q.put(PE, ([D["sk", j], m_id] + bank_free[f"Y{j}"]) if s == 0 else [], lambda e, j=j, s=s, bk=bk: e.transpose(
                        bk[:, seg(s)], sk[:, j, seg(s)], ident[:, :]), "pe_kt" if s == 2 else None)
                a = Q.put(AC, [m] + D.get(("u2", n - 1), []), lambda e, j=j, bk=bk: e.activation(
                    kn[:, j, :, :], bk[:, 0:384].rearrange("p (s k) -> p s k", s=3), ACT.Copy), "a_kn")
                D["kn", j] = a
                bank_free[f"Y{j}"] = [a]
            for j in range(2):
                bk = banks[f"X{j}"]
                for s in range(NSEG):
                    m = Q.put(PE, ([D["q", j], D["k", j]] + bank_free[f"X{j}"]) if s == 0 else [], lambda e, j=j, s=s, bk=bk: e.matmul(
                        bk[:, seg(s)], qT[:, j, seg(s)], kT[:, j, seg(s)], start=True, stop=True), "pe_s" if s == 3 else None)
                D["scores"] = [m]
                for s in range(NSEG):
                    w = [m, m_mk] + D.get("at", []) + list(m_beta[0:2])
                    t = Q.put(DV, w if s == 0 else [], lambda e, j=j, s=s, bk=bk: e.tensor_tensor_reduce(
                        S[:, j, seg(s)], bk[:, seg(s)], mask[:, :], 1.0, NEG, ALU.add, ALU.max,
                        st[:, 0, j, s:s + 1]), "v_mx")
                bank_free[f"X{j}"] = [t]
                t = Q.put(DV, [t] + D.get(("exp", j), []), lambda e, j=j: e.tensor_scalar(
                    st[:, 1, j, :], st[:, 0, j, :], -SCALE, None, ALU.mult), "v_mx")
                for s in range(NSEG):
                    a = Q.put(AC, [t] + D.get("rd", []), lambda e, j=j, s=s: e.activation(
                        S[:, j, seg(s)], S[:, j, seg(s)], ACT.Exp, bias=st[:, 1, j, s:s + 1], scale=SCALE,
                        accum_out=st[:, 2, j, s:s + 1]), "a_p")
                D["exp", j] = [a]

        def update(n, s):
            for j in range(2):
                bk = banks[f"Z{j}"]
                rhs = v[n % 2][:, 0, j, :] if s == 0 else delta[:, j, :]
                w = [D["kn", j], m_beta[2]] + ([D["v", n, 0]] if s == 0 else [D["delta", j]])
                m = Q.put(PE, w + bank_free[f"Z{j}"], lambda e, j=j, bk=bk, rhs=rhs: e.matmul(
                    bk[:, 258:387], kn[:, j, s, :], rhs, start=True, stop=True), "pe_u")
                prev = mem0[:, :] if s == 0 else mem[:, j, :]
                t = Q.put(DV, [m] + D.get("am", []) + D.get(("mem", j), []), lambda e, j=j, bk=bk, prev=prev: e.tensor_tensor(
                    mem[:, j, :], bk[:, 258:387], prev, ALU.add), "v_mem")
                bank_free[f"Z{j}"] = [t]
                D["mem", j] = [t]
            if s == 2:
                D["u2", n] = [m]

        def recall(n, s):
            for j in range(2):
                bk = banks[f"Z{j}"]
                w = bank_free[f"Z{j}"] + D["mem", j] + [D["sq", j]]
                if s < 3:
                    Q.put(PE, w, lambda e, j=j, bk=bk: e.matmul(
                        bk[:, 0:129], sk[:, j, seg(s)], mem[:, j, :], start=True, stop=True))
                m = Q.put(PE, w, lambda e, j=j, bk=bk: e.matmul(
                    bk[:, 129:258], sq[:, j, seg(s)], mem[:, j, :], start=True, stop=True), "pe_am")
                lo = 0 if s < 3 else 1
                t = Q.put(DV, [m] + D.get(("rz", j), []), lambda e, j=j, bk=bk, lo=lo: e.reciprocal(
                    rz[:, j, lo:2], bk[:, 128 + 129 * lo:258:129]), "v_r")
                r = t
                if s < 3:
                    t = Q.put(DV, [r, D["v", n, 0], D["v", n, 1]], lambda e, j=j, bk=bk: e.scalar_tensor_tensor(
                        delta[:, j, 0:P], bk[:, 0:128], rz[:, j, 0:1], v[n % 2][:, s, j, 0:P], ALU.mult, ALU.subtract,
                        reverse1=True), "v_r")
                    D["delta", j] = t
                t = Q.put(DV, [r, D["bet"]], lambda e, j=j, bk=bk: e.scalar_tensor_tensor(
                    t2[:, j, s - 1, :], bk[:, 129:257], rz[:, j, 1:2], bet[:, 128 * j:128 * j + 128],
                    ALU.mult, ALU.mult), "v_r")
                bank_free[f"Z{j}"] = [t]
                D["rz", j] = [t]
                D["t2", j, s] = t
            D["am"] = [m]
            if s == 3:
                D["am3"] = [m]
                D["t2_3"] = [t]
            if s == 2:
                D["dk2"] = [m]

        def turn_p(n):
            for j in range(2):
                bk = banks[f"Y{j}"]
                for s in range(NSEG):
                    m = Q.put(PE, (D["exp", j] + [m_id] + bank_free[f"Y{j}"]) if s == 0 else [], lambda e, j=j, s=s, bk=bk: e.transpose(
                        bk[:, seg(s)], S[:, j, seg(s)], ident[:, :]), "pe_pt" if s == 3 else None)
                a = Q.put(AC, [m] + D.get("pv", []), lambda e, j=j, bk=bk: e.activation(
                    pT[:, j, :], bk[:, :], ACT.Copy), "a_pt")
                D["pT", j] = a
                D["p_read", j] = m
                bank_free[f"Y{j}"] = [a]
            D["rd"] = [Q.put(DV, D["exp", 1] + D["exp", 0], lambda e: e.reciprocal(
                st[:, 3, :, :], st[:, 2, :, :]), "v_rd")]

        def pv(n):
            for j in range(2):
                bk = banks[f"X{j}"]
                for s in range(NSEG):
                    m = Q.put(PE, ([D["pT", j], D["vs"]] + bank_free[f"X{j}"]) if s == 0 else [], lambda e, j=j, s=s, bk=bk: e.matmul(
                        bk[:, seg(s)], pT[:, j, seg(s)], vs[:, s, j, :], start=True, stop=True), "pe_pv" if s == 3 else None)
                D["ad", j] = m
            D["pv"] = [m]

        def join(n, s):
            for j in range(2):
                bk = banks[f"X{j}"]
                w = [D["ad", j], D["p_read", j]] + D["rd"]
                if s == 0:
                    t = Q.put(DV, w, lambda e, j=j, bk=bk: e.tensor_scalar(
                        S[:, j, seg(0)], bk[:, seg(0)], st[:, 3, j, 0:1], None, ALU.mult), "v_at")
                else:
                    t = Q.put(DV, w + [D["t2", j, s]], lambda e, j=j, bk=bk: e.scalar_tensor_tensor(
                        S[:, j, seg(s)], bk[:, seg(s)], st[:, 3, j, s:s + 1], t2[:, j, s - 1, :],
                        ALU.mult, ALU.add), "v_at")
                bank_free[f"X{j}"] = [t]
                D["join", j] = t

        def turn_att(n):
            if n % 4 == 0:
                D["att"] = []
            for j in range(2):
                bk = banks[f"Y{j}"]
                for s in range(NSEG):
                    m = Q.put(PE, ([D["join", j]] + bank_free[f"Y{j}"]) if s == 0 else [], lambda e, j=j, s=s, bk=bk: e.transpose(
                        bk[:, seg(s)], S[:, j, seg(s)], ident[:, :]), "pe_at" if s == 3 else None)
                D["at"] = [m]
                h = 2 * (n % 4) + j
                turned = bk[:, :].rearrange("p (s j) -> p j s", j=16)
                hi, lo = ah[:, :, 32 * h:32 * h + 32], al[:, :, 32 * h:32 * h + 32]
                a = Q.put(AC, [m] + D.get("wo", []), lambda e, hi=hi, turned=turned: e.activation(hi, turned, ACT.Copy), "a_at")

                def low(j=j, a=a, hi=hi, lo=lo, turned=turned):
                    t = Q.put(DV, [a], lambda e: e.tensor_tensor(lo, turned, hi, ALU.subtract), "v_al")
                    bank_free[f"Y{j}"] = [t]
                    D["att"] = D["att"] + [a, t]

                before.append(low)

        z_ready = {}
        F = {}
        rt_free, sg_free = {}, {}

        def modulate(b, bar=None):
            z_ready[b] = []
            M = {}

            def load():
                if not rt_free:
                    w = [Q.last[DV, "v_h"], Q.last[AC, "a_ho"], Q.last[PE, "pe_h"],
                         Q.last[AC, "a_h"], Q.last[SP, "d_ho"]]
                    rt_free.update({i: w for i in range(2)})
                    sg_free.update({i: w for i in range(6)})
                for c in range(NC):
                    M["sg", c] = Q.dma(sg_free[c] + [m_x1[b]], sg[c][:, :], x1_s[b, :, c, :], f"d_sg{c}")
                for c in range(2):
                    ratio(c)

            def ratio(c):
                s = c % 2
                M["rt", c] = Q.dma(rt_free[s] + [m_ratio[b, c]], rt[s][:, :], ratio_s[b, c], f"d_rt{s}")

            def sigmoid():
                for c in range(NC):
                    M["a", c] = Q.put(AC, [M["sg", c]], lambda e, c=c: e.activation(
                        sg[c][:, :], sg[c][:, :], ACT.Sigmoid), "a_z")

            def times(c):
                s = c % 2
                M["t", c] = Q.put(DV, [M["a", c], M["rt", c]], lambda e: e.tensor_tensor(
                    sg[c][:, :], sg[c][:, :], rt[s][:, :], ALU.mult), "v_z")
                rt_free[s] = [M["t", c]]
                if c < 2:
                    ratio(c + 2)

            def parts(c):
                w = y_free[4 + b] if bar is None else bar
                h = Q.put(AC, [M["t", c]] + w, lambda e: e.activation(zh[b][:, c, :], sg[c][:, :], ACT.Copy), "a_z")
                l = Q.put(PL, [M["t", c], h] + w, lambda e: e.tensor_tensor(
                    zl[b][:, c, :], sg[c][:, :], zh[b][:, c, :], ALU.subtract), "p_z")
                sg_free[c] = [l, h]
                z_ready[b] += [h, l]

            return ([(1500, load), (1500, wait), (1500, wait), (1500, sigmoid), (1500, wait)]
                    + [(1000, lambda c=c: times(c)) for c in range(NC)],
                    [(800, lambda c=c: parts(c)) for c in range(NC)])

        background += [(cost, fn, len(tiles) + 1) for part in modulate(0) for cost, fn in part]
        background += [(cost, fn, len(tiles) + 2) for part in modulate(1) for cost, fn in part]

        ffn = [(g, b) for g in range(NG) for b in range(NB)]
        bar = []
        names = list(banks)
        bi = [0]

        def next_bank():
            bi[0] += 1
            return names[bi[0] % 8]

        sgi = [0]
        h_used = {0: [], 1: bar}
        U = {}

        def up_part(n, bank_of, j, k):
            g, b = ffn[n]
            last = n + 1 == len(ffn) or ffn[n + 1][0] != g
            wi = windex[k, g]
            slot = W["slot"][wi]
            U["bank", k] = bank_of()
            bk = banks[U["bank", k]]
            assert len(z_ready[b]) == 2 * NC
            terms = [((wh[slot][:, 256 * c + 128 * j:256 * c + 128 * j + 128],
                       wl[slot][:, 256 * c + 128 * j:256 * c + 128 * j + 128]),
                      (zh[b][:, c, :], zl[b][:, c, :])) for c in range(NC)]
            U[k] = passes(U["bank", k], bk[:, :], terms, W["ready"][wi] + z_ready[b], "pe_g")
            if last and j == 1:
                W["free"].append((slot, [U[k]]))
            if k == "1":
                U["s"] = s = 4 + sgi[0] % 2 if n == 0 else sgi[0] % 6
                sgi[0] += 1
                t_ = sg[s]
                a = Q.put(AC, [U["1"]] + sg_free[s], lambda e: e.activation(t_[:, :], bk[:, :], ACT.Sigmoid), "a_f")
                U["t"] = Q.put(DV, [a], lambda e: e.tensor_tensor(t_[:, :], bk[:, :], t_[:, :], ALU.mult), "v_f")
                bank_free[U["bank", "1"]] = [U["t"]]
                return
            s = U["s"]
            t_ = sg[s]
            t = Q.put(DV, [U["t"], U["3"]], lambda e: e.tensor_tensor(t_[:, :], bk[:, :], t_[:, :], ALU.mult), "v_f")
            bank_free[U["bank", "3"]] = [t]
            o = n % 2
            h = Q.put(AC, [t] + h_used[o], lambda e: e.activation(hh[o][:, j, :], t_[:, :], ACT.Copy), "a_f")
            l = Q.put(PL, [h, t] + h_used[o], lambda e: e.tensor_tensor(
                hl[o][:, j, :], t_[:, :], hh[o][:, j, :], ALU.subtract), "p_f")
            sg_free[s] = [l, h]
            F.setdefault(n, []).extend([h, l])

        def up(n):
            for j in range(2):
                for k in "13":
                    up_part(n, next_bank, j, k)
                split_weights(1)

        a_min(0)
        b_min(0)
        a_exp(0)
        a_mul(0)
        b_exp(0)
        b_mul(0)
        e_exp(0)
        m_beta = early_constants()
        load_halves()
        work_until(0)
        split_weights(1)
        work_until(1)
        split_weights(1)
        work_until(2)
        split_weights(1)
        work_until(3)
        load_bet(0)
        for half in range(2):
            for part in range(2):
                vv(0, half, part)
        v_scaled(0)
        for which in "kq":
            for j in range(2):
                for part in range(2):
                    kq(0, which, j, part)
                behind.pop(0)()
        split_weights(2)

        def now(steps):
            for fn in steps:
                fn()

        bg = BG

        ups = {"k00": (0, "1"), "k10": (0, "3"), "q00": (1, "1"), "q10": (1, "3")}

        def fill(n, what, ns):
            due = behind[:]
            behind.clear()
            if later:
                later.pop(0)()
            if n < len(order):
                if what[0] == "v":
                    vv(n, int(what[1]), int(what[2]))
                    if what == "v11":
                        D["vs_due"] = n
                else:
                    kq(n, what[0], int(what[1]), int(what[2]))
            elif what in ups:
                work_until(len(tiles) + 1)
                up_part(0, next_g, *ups[what])
            split_weights(1)
            while before:
                before.pop(0)()
            if at[0] == 0 or background[at[0] - 1][2] >= len(tiles):
                ns = max(ns, LATE)
            whole[0] = what[-1] == "1" or n == len(order)
            work(ns)
            whole[0] = False
            now(due)

        for n in range(len(order)):
            nx = n + 1
            if nx < len(order):
                b = order[nx][1]
                if b not in y_ready or len(y_ready[b]) < 2 * NC:
                    work_until([i for i, t in enumerate(tiles) if t == (0, b, NC - 1)][0])
            burst = n % 4 == 0 and n > 0
            pieces = ["v00", "v01", "v10", "v11", "k00", "k01", "k10", "k11", "q00", "q01", "q10", "q11"]
            todo = [0]

            def between(k):
                if burst:
                    if todo[0] < 8:
                        due = behind[:]
                        behind.clear()
                        wo(n - 1, todo[0])
                        split_weights(1)
                        work(BURST[todo[0]])
                        todo[0] += 1
                        now(due)
                else:
                    for _ in range(k):
                        fill(nx, pieces[todo[0]], STEADY[todo[0]])
                        todo[0] += 1

            if n > 0:
                load_bet(n)
            s1(n)
            between(1)
            update(n, 0)
            between(1)
            recall(n, 1)
            between(2)
            turn_p(n)
            update(n, 1)
            between(1)
            recall(n, 2)
            pv(n)
            join(n, 0)
            if nx < len(order) and not burst:
                v_scaled(nx)
            between(2)
            update(n, 2)
            join(n, 1)
            between(1)
            join(n, 2)
            recall(n, 3)
            join(n, 3)
            between(2)
            if burst:
                while todo[0] < 8:
                    between(1)
            turn_att(n)
            if n == len(order) - 1:
                between(2)
                now(behind)
                behind.clear()
            elif burst:
                for p in pieces:
                    fill(nx, p, AFTER)
                    if p == "v11" and nx < len(order):
                        v_scaled(nx)
            else:
                between(2)
            whole[0] = True
            work(bg)
            whole[0] = False
        for i in range(8):
            split_weights(1)
            wo(len(order) - 1, i)
            work(3 * bg)
            if i == 3:
                work_until(len(tiles) + 2)
                z2 = modulate(2, bar)
                now(fn for _, fn in z2[0])
        bar[:] = list(Q.last.values())
        split_weights(3)
        m_x = {}

        def load_x(b):
            m_x[b] = Q.dma(bar + [m_x1[b]], x[:, b, :, :], x1_s[b], f"d_xx{b}")

        def down(n):
            g, b = ffn[n]
            last = n + 1 == len(ffn) or ffn[n + 1][0] != g
            wi = windex["2", g]
            slot = W["slot"][wi]
            o = n % 2
            for dc in range(NC):
                bank = next_bank()
                terms = [((wh[slot][:, 512 * j + 128 * dc:512 * j + 128 * dc + 128],
                           wl[slot][:, 512 * j + 128 * dc:512 * j + 128 * dc + 128]),
                          (hh[o][:, j, :], hl[o][:, j, :])) for j in range(2)]
                m = passes(bank, banks[bank][:, :], terms, W["ready"][wi] + F[n], "pe_g")
                a = Q.put(DV, [m, m_x[b]], lambda e, bank=bank, dc=dc: e.tensor_tensor(
                    x[:, b, dc, :], x[:, b, dc, :], banks[bank][:, :], ALU.add), "v_x")
                bank_free[bank] = [a]
                if g == NG - 1:
                    outs.append(Q.dma([a], out_d[b, :, dc, :], x[:, b, dc, :], "d_out"))
            h_used[o] = [m]
            if last:
                W["free"].append((slot, [m]))
                split_weights(2)

        outs = []
        for n in range(len(ffn) + 1):
            if 0 < n < len(ffn):
                up(n)
            if n == 0:
                load_x(0)
                now(fn for _, fn in z2[1])
            if n == 1:
                z3 = modulate(3, bar)
                now(fn for _, fn in z3[0])
                now(fn for _, fn in z3[1])
                for b in (1, 2, 3):
                    load_x(b)
            if n > 0:
                down(n - 1)
        Q.put(SP, [outs[-1]], None)

        Q.run(ctx.enter_context(nc.Block()))


_OUT = (NB, P, NC, T)


def kernel(x, fside_BxSxS_0, cond_512, L0_cond_w, L0_cond_u, L0_attn_Wq, L0_attn_Wk, L0_attn_Wv, L0_attn_Wo,
           L0_attn_betas, L0_cond2_w, L0_cond2_u, L0_ffn_W1, L0_ffn_W2, L0_ffn_W3):
    import numpy as np
    import concourse.bacc as bacc
    from concourse.bass_utils import run_bass_kernel_spmd as run

    def fresh(a):
        return np.ascontiguousarray(a)

    def channels(a):
        a = np.asarray(a).reshape(NB, T, NC, P)
        return fresh(a.transpose(0, 3, 2, 1))

    def columns(w):
        a = np.asarray(w).reshape(NC, P, NG, 256)
        return fresh(a.transpose(2, 1, 0, 3)).reshape(NG, P, 2, 512)

    ident = np.eye(P, dtype=np.float32)
    mask = np.where(np.tril(np.ones((P, P), bool)), np.float32(0), np.float32(NEG)).astype(np.float32)
    had = np.ones((1, 1), np.float32)
    while had.shape[0] < P:
        had = np.block([[had, had], [had, -had]]).astype(np.float32)
    wo = fresh(np.asarray(L0_attn_Wo).reshape(NG, 2, P, C).transpose(0, 2, 1, 3))
    w2 = np.asarray(L0_ffn_W2).T.reshape(16, P, 8, 64)
    wu = np.stack([np.asarray(a).reshape(NC, P).T for a in (L0_cond_w, L0_cond_u, L0_cond2_w, L0_cond2_u)], 1)
    arrays = {
        "xT": channels(x), "fT": channels(fside_BxSxS_0),
        "cond": fresh(np.asarray(cond_512).reshape(1, NB * P)), "wu": fresh(wu),
        "wq": columns(L0_attn_Wq), "wk": columns(L0_attn_Wk), "wv": columns(L0_attn_Wv),
        "wo": wo, "betas": fresh(np.asarray(L0_attn_betas).reshape(H, P)),
        "w1": columns(np.asarray(L0_ffn_W1).T), "w3": columns(np.asarray(L0_ffn_W3).T),
        "w2": fresh(w2.transpose(2, 1, 0, 3)), "ident": ident, "mask": mask, "had": had,
    }
    nc = bacc.Bacc("TRN2", target_bir_lowering=False, num_devices=1)
    args = [nc.dram_tensor("in_" + k, list(a.shape), F32, kind="ExternalInput").ap() for k, a in arrays.items()]
    args.append(nc.dram_tensor("out_0", list(_OUT), F32, kind="ExternalOutput").ap())
    adaln_attn_ffn(nc, *args)
    r = run(nc, [{"in_" + k: a for k, a in arrays.items()}], core_ids=[0])
    got = np.asarray(r.results[0]["out_0"])
    return np.ascontiguousarray(got.transpose(0, 3, 2, 1)).reshape(NB, T, C)
```

```python
from contextlib import ExitStack

import concourse.bass as bass
from concourse import mybir

F32 = mybir.dt.float32
F32R = mybir.dt.float32r
ALU = mybir.AluOpType
ACT = mybir.ActivationFunctionType
AX_X = mybir.AxisListType.X

P = 128
NB = 4
T = 512
C = 512
NC = C // P
H = 16
SEG = 128
NSEG = T // SEG
NG = 8
NRING = 6
NSTAGE = 4
HI_ACT = "ovk"
STEADY = [0, 700, 700, 0, 700, 700, 700, 700, 700, 700, 700, 0]
BURST = [700] * 8
AFTER = 900
LATE = 1200
END = 750
HID = 2048
SCALE = float(P) ** -0.5
RSQ = float(HID) ** -0.5
NEG = -3.0e38
PE, DV, AC, PL, SP = "tensor", "vector", "scalar", "gpsimd", "sync"


class Queues:

    def __init__(self, nc, ctx):
        self.nc, self.ctx = nc, ctx
        self.todo = {e: [] for e in (PE, DV, AC, PL, SP)}
        self.sems, self.count, self.seen = {}, {}, {}
        self.last = {}

    def step(self, name, by):
        if name not in self.sems:
            self.sems[name] = self.ctx.enter_context(self.nc.semaphore(name))
            self.count[name] = 0
        self.count[name] += by
        return name, self.count[name]

    def put(self, eng, waits, fn, name=None, by=1):
        need = []
        for n, v in waits:
            if self.seen.get((eng, n), 0) < v:
                self.seen[(eng, n)] = v
                need = [x for x in need if x[0] != n] + [(n, v)]
        mark = self.step(name, by) if name else None
        if mark:
            self.last[(eng, name)] = mark
        self.todo[eng].append((need, fn, name, by))
        return mark

    def dma(self, waits, out, in_, name):
        return self.put(SP, waits, lambda e: e.dma_start(out, in_), name, 16)

    def dma_by_scalar(self, waits, out, in_, name):
        return self.put(AC, waits, lambda e: e.dma_start(out, in_), name, 16)

    def run(self, block):
        def program(todo):
            def body(e):
                for need, fn, name, by in todo:
                    for n, v in need:
                        e.wait_ge(self.sems[n], v)
                    if fn is None:
                        continue
                    ins = fn(e)
                    if name:
                        ins.then_inc(self.sems[name], by)
            return body
        block.tensor(program(self.todo[PE]))
        block.vector(program(self.todo[DV]))
        block.scalar(program(self.todo[AC]))
        block.gpsimd(program(self.todo[PL]))
        block.sync(program(self.todo[SP]))


def adaln_attn_ffn(nc, xT_d, fT_d, cond_d, wu_d, wq_d, wk_d, wv_d, wo_d, betas_d,
                   w1_d, w3_d, w2_d, ident_d, mask_d, had_d, out_d):
    beta_s = nc.dram_tensor("beta_s", [2, H, P], F32).ap()
    ratio_s = nc.dram_tensor("ratio_s", [NB, NC, P, T], F32).ap()
    x1_s = nc.dram_tensor("x1_s", [NB, P, NC, T], F32).ap()
    w2_s = nc.dram_tensor("w2_s", [8, P, 16, 64], F32).ap()

    with ExitStack() as ctx:
        Q = Queues(nc, ctx)

        def sb(stack, name, shape, dt=F32):
            return stack.enter_context(nc.sbuf_tensor(name, shape, dt))

        banks = {n: ctx.enter_context(nc.psum_tensor("ps" + n, [P, 512], F32))
                 for n in ("G0", "G1", "X0", "X1", "Y0", "Y1", "Z0", "Z1")}

        yh = [sb(ctx, f"yh{i}", [P, NC, T], F32R) for i in range(2)]
        yl = [sb(ctx, f"yl{i}", [P, NC, T], F32R) for i in range(2)]
        wh = [sb(ctx, f"wh{i}", [P, 1024], F32R) for i in range(NRING)]
        wl = [sb(ctx, f"wl{i}", [P, 1024], F32R) for i in range(NRING)]
        stage = [sb(ctx, f"stage{i}", [P, 512]) for i in range(NSTAGE)]
        wu = sb(ctx, "wu", [P, 4, NC])
        ucut = sb(ctx, "ucut", [P, 2, NC])
        dec0 = sb(ctx, "dec0", [P, 2, NC])
        dec = sb(ctx, "dec", [P, NB, 2, NC])
        tf = sb(ctx, "tf", [P, 4, NB])

        two = ExitStack()
        kx = [sb(two, f"kx{i}", [P, T]) for i in range(2)]
        EK, EKV, EU, EUV, NF, DF, ER, OY = (
            sb(two, n, [P, T]) for n in ("EK", "EKV", "EU", "EUV", "NF", "DF", "ER", "OY"))
        NBK = sb(two, "NBK", [P, T + 1])
        DBK = sb(two, "DBK", [P, T + 1])
        two.close()
        three = ExitStack()
        HA, HB, HO = (sb(three, n, [P, 1024]) for n in ("HA", "HB", "HO"))
        HH = sb(three, "HH", [P, 1024], F32R)
        HL = sb(three, "HL", [P, 1024], F32R)
        hadf = sb(three, "hadf", [P, P])
        had = sb(three, "had", [P, P], F32R)
        three.close()
        sg = [sb(ctx, f"sg{i}", [P, T]) for i in range(6)]
        rt = [sb(ctx, f"rt{i}", [P, T]) for i in range(2)]
        hh = [sb(ctx, "hh0", [P, 2, T], F32R)]
        hl = [sb(ctx, "hl0", [P, 2, T], F32R)]
        sb(ctx, "pad", [P, 32])

        one = ExitStack()
        xb = sb(one, "xb", [P, NC, T])
        ah = sb(one, "ah", [P, 16, 256], F32R)
        al = sb(one, "al", [P, 16, 256], F32R)
        qT = sb(one, "qT", [P, 2, T])
        kT = sb(one, "kT", [P, 2, T])
        sq = sb(one, "sq", [P, 2, T])
        sk = sb(one, "sk", [P, 2, T])
        v = [sb(one, f"v{i}", [P, NSEG, 2, P + 1]) for i in range(2)]
        vs = sb(one, "vs", [P, NSEG, 2, P])
        S = sb(one, "S", [P, 2, T])
        pT = sb(one, "pT", [P, 2, T])
        kn = sb(one, "kn", [P, 2, 3, P])
        t2 = sb(one, "t2", [P, 2, 3, P])
        mem = sb(one, "mem", [P, 2, P + 1])
        mem0 = sb(one, "mem0", [P, P + 1])
        delta = sb(one, "delta", [P, 2, P + 1])
        bet = sb(one, "bet", [P, 256])
        omb = sb(one, "omb", [P, 256])
        etmps = [sb(one, f"etmp{i}", [P, T]) for i in range(2)]
        ident = sb(one, "ident", [P, P])
        mask = sb(one, "mask", [P, P])
        st = sb(one, "st", [P, 4, 2, NSEG])
        rz = sb(one, "rz", [P, 2, 2])
        one.close()
        x = sb(ctx, "x", [P, NB, NC, T])
        zh = yh + [sb(ctx, f"zh{i}", [P, NC, T], F32R) for i in (2, 3)]
        zl = yl + [sb(ctx, f"zl{i}", [P, NC, T], F32R) for i in (2, 3)]
        hh += [sb(ctx, "hh1", [P, 2, T], F32R)]
        hl += [sb(ctx, "hl1", [P, 2, T], F32R)]

        cb = S[:, 0, :]
        bt = S[0:H, 1, 0:P]
        m_cb = Q.dma([], cb, cond_d.to_broadcast([P, NB * P]), "d_cb")
        m_wu = Q.dma([], wu[:, :, :], wu_d, "d_wu")
        m_kx = {}
        for i in range(2):
            m_kx[i] = Q.dma([], kx[i][:, :], fT_d[0, :, i, :], f"d_k{i}")
        m_bt = Q.dma([], bt, betas_d, "d_bt")
        m_er = {c: Q.dma([], t, xT_d[0, :, c, :], f"d_er{c}") for c, t in enumerate(
            (ER[:, :], etmps[0][:, :], etmps[1][:, :], pT[:, 0, :]))}
        order = [(g, b) for b in range(NB) for g in range(NG)]
        stream, windex = [], {}

        def streamed(k, g, key):
            windex[k, key] = len(stream)
            stream.append((k, g))

        for n in range(-1, len(order)):
            if n >= 0 and n % 4 == 0 and n > 0:
                for i in range(8):
                    streamed("o", i, (n - 1, i))
            if n + 1 < len(order):
                for k in "vkq":
                    streamed(k, order[n + 1][0], n + 1)
        streamed("1", 0, 0)
        streamed("3", 0, 0)
        for i in range(8):
            streamed("o", i, (len(order) - 1, i))
        streamed("2", 0, 0)
        for g in range(1, NG):
            for k in "132":
                streamed(k, g, g)
        src = {"q": wq_d, "k": wk_d, "v": wv_d, "o": wo_d, "1": w1_d, "3": w3_d}
        W = {"next": 0, "load": 0, "split": 0, "half": [], "ready": {}, "slot": {},
             "free": [(i, []) for i in range(NRING)]}
        stage_free = [[] for _ in range(NSTAGE)]
        m_w2s = []

        def load_halves():
            while W["load"] < 2 * len(stream) and W["load"] < W["split"] + NSTAGE:
                i, half = divmod(W["load"], 2)
                k, g = stream[i]
                if k == "2" and not m_w2s:
                    return
                s = W["load"] % NSTAGE
                if k == "2":
                    out = stage[s][:, :].rearrange("p (n a d) -> p n a d", n=4, a=2)
                    in_ = w2_s[4 * half:4 * half + 4, :, 2 * g:2 * g + 2, :].rearrange("n p a d -> p n a d")
                    m = Q.dma(stage_free[s] + m_w2s, out, in_, f"d_w{s}")
                else:
                    m = Q.dma(stage_free[s], stage[s][:, :], src[k][g, :, half, :], f"d_w{s}")
                W["half"].append(m)
                W["load"] += 1

        def split_weights(limit=1):
            n = 0
            while W["next"] < len(stream) and n < limit:
                i = W["next"]
                k = stream[i][0]
                if not W["free"]:
                    return
                load_halves()
                if W["load"] < 2 * i + 2 and k == "2" and not m_w2s:
                    return
                slot, free = W["free"].pop(0)
                W["slot"][i] = slot
                marks = []
                for half in range(2):
                    s = (2 * i + half) % NSTAGE
                    m_in = W["half"][2 * i + half]
                    if k == "2":
                        hi = wh[slot][:, :].rearrange("p (a n d) -> p n a d", a=2, n=8)[:, 4 * half:4 * half + 4]
                        lo = wl[slot][:, :].rearrange("p (a n d) -> p n a d", a=2, n=8)[:, 4 * half:4 * half + 4]
                        raw = stage[s][:, :].rearrange("p (n a d) -> p n a d", n=4, a=2)
                    else:
                        hi = wh[slot][:, 512 * half:512 * half + 512]
                        lo = wl[slot][:, 512 * half:512 * half + 512]
                        raw = stage[s][:, :]
                    if k in HI_ACT or i < 3:
                        a = Q.put(AC, [m_in] + free, lambda e, hi=hi, raw=raw: e.activation(hi, raw, ACT.Copy), "a_wh")
                    else:
                        a = Q.put(PL, [m_in] + free, lambda e, hi=hi, raw=raw: e.tensor_scalar(
                            hi, raw, 1.0, 0.0, ALU.mult, ALU.add), "p_wh")
                    p = Q.put(PL, [a, m_in] + free, lambda e, lo=lo, raw=raw, hi=hi: e.tensor_tensor(
                        lo, raw, hi, ALU.subtract), "p_wl")
                    stage_free[s] = [a, p]
                    marks += [a, p]
                    W["split"] += 1
                    load_halves()
                    if half == 0 and W["load"] < 2 * i + 2:
                        raise AssertionError("a weight's second half is not there")
                W["next"] = i + 1
                W["ready"][i] = marks
                n += 1

        bank_free = {n: [] for n in banks}

        def passes(bank, out, terms, waits, name, part=(0, 1), free=True):
            k, n = part
            if free and k == 0:
                waits = waits + bank_free[bank]
            pairs = [p for (lh, ll), (rh, rl) in terms for p in ((lh, rh), (lh, rl), (ll, rh))]
            first, end = k * len(pairs) // n, (k + 1) * len(pairs) // n
            for i in range(first, end):
                a, c = pairs[i]
                m = Q.put(PE, waits if i == first else [], lambda e, a=a, c=c, i=i: e.matmul(
                    out, a, c, start=(i == 0), stop=(i == len(pairs) - 1)), name if i == len(pairs) - 1 else None)
            return m

        y_ready = {}
        y_free = {0: [], 1: []}
        tiles = [(i, b, c) for i, b in ((0, 0), (0, 1), (1, 0), (0, 2), (1, 1), (0, 3), (1, 2), (1, 3)) for c in range(NC)]
        B = {"EK": [], "EU": {0: [], 1: []}, "N": {0: [], 1: []}, "kfree": {0: [], 1: []}, "ER": [], "OY": []}
        m_ratio = {}
        A = {n: {} for n in range(len(tiles) + 1)}
        firsts = [n for n, t in enumerate(tiles) if t[0] == 0]

        nbk1 = sq[:, :, :].rearrange("p a t -> p (a t)")
        dbk1 = sk[:, :, :].rearrange("p a t -> p (a t)")
        sets = [(NF[:, :], DF[:, :], NBK[:, :], DBK[:, :]), (qT[:, 0, :], qT[:, 1, :], nbk1, dbk1)]

        eus = [(EU[:, :], EUV[:, :]), (kT[:, 0, :], kT[:, 1, :])]
        ers = [ER[:, :], etmps[0][:, :], etmps[1][:, :], pT[:, 0, :]]

        def which(n):
            return n % 2 if n < 4 else 0

        def k_load(n):
            if 2 <= n < len(tiles):
                _, b, c = tiles[n]
                m_kx[n] = Q.dma_by_scalar(B["kfree"][n % 2], kx[n % 2][:, :], fT_d[b, :, c, :], f"d_k{n % 2}")

        def er_load(n):
            if n in firsts and n > 0:
                _, b, c = tiles[n]
                m_er[n] = Q.dma_by_scalar(B["ER"], ER[:, :], xT_d[b, :, c, :], "d_er0")

        def a_min(n):
            if n < len(tiles):
                k = kx[n % 2][:, :]
                A[n]["mn"] = Q.put(DV, [m_kx[n]] + B["EK"], lambda e: e.tensor_scalar(EK[:, :], k, 30.0, None, ALU.min), "v_sc")

        def a_exp(n):
            if n < len(tiles):
                A[n]["ek"] = Q.put(AC, [A[n]["mn"]], lambda e: e.activation(EK[:, :], EK[:, :], ACT.Exp), "a_ek")

        def a_mul(n):
            if n < len(tiles):
                k = kx[n % 2][:, :]
                A[n]["ekv"] = Q.put(PL, [A[n]["ek"]] + B["EK"], lambda e: e.tensor_tensor(EKV[:, :], EK[:, :], k, ALU.mult), "p_ekv")

        def b_min(n):
            if n < len(tiles):
                k, (i, b, c) = kx[n % 2][:, :], tiles[n]
                eu, w = eus[which(n)][0], which(n)
                A[n]["mu"] = Q.put(DV, [m_kx[n], m_cut] + B["EU"][w], lambda e: e.tensor_scalar(
                    eu, k, ucut[:, i, c:c + 1], None, ALU.min), "v_sc")

        def b_exp(n):
            if n < len(tiles):
                i, b, c = tiles[n]
                eu = eus[which(n)][0]
                A[n]["eu"] = Q.put(AC, [A[n]["mu"]], lambda e: e.activation(
                    eu, eu, ACT.Exp, bias=wu[:, 2 * i + 1, c:c + 1]), "a_eu")

        def b_mul(n):
            if n < len(tiles):
                k, w = kx[n % 2][:, :], which(n)
                eu, euv = eus[w]
                A[n]["euv"] = Q.put(PL, [A[n]["eu"]] + B["EU"][w], lambda e: e.tensor_tensor(euv, eu, k, ALU.mult), "p_euv")
                B["kfree"][n % 2] = [A[n]["euv"], A[n]["ekv"]]

        def e_exp(n):
            if n in firsts:
                er = ers[n if n < 4 else 0]
                a = Q.put(AC, [m_er[n]], lambda e: e.activation(er, er, ACT.Exp, scale=-1.0), "a_er")
                A[n]["er"] = Q.put(PL, [a], lambda e: e.tensor_scalar(er, er, 1.0, 1.0, ALU.mult, ALU.add), "p_er")

        def scan_steps(n):
            i, b, c = tiles[n]
            d = dec[:, b, i, c:c + 1]
            db = d.to_broadcast([P, T])
            M = {}
            early = n < 4
            set_ = n % 2 if early else 0
            nf, df, nbk, dbk = sets[set_]
            (eu, euv), er = eus[set_], ers[n if early else 0]
            after = ([f for f in firsts if f > n] or [None])[0]

            def s1():
                k_load(n + 2)
                M["nf"] = Q.put(DV, [A[n]["ekv"], m_dec, m_nb0] + B["N"][set_], lambda e: e.tensor_tensor_scan(
                    nf, db, EKV[:, :], 0.0, ALU.mult, ALU.add), "v_sc")

            def s2():
                M["nb"] = Q.put(DV, [A[n]["ekv"]], lambda e: e.tensor_tensor_scan(
                    nbk[:, T - 1::-1], db, EKV[:, ::-1], 0.0, ALU.mult, ALU.add), "v_sc")

            def s3():
                M["df"] = Q.put(DV, [A[n]["ek"]], lambda e: e.tensor_tensor_scan(
                    df, db, EK[:, :], 0.0, ALU.mult, ALU.add), "v_sc")

            def s4():
                M["db"] = Q.put(DV, [A[n]["ek"]], lambda e: e.tensor_tensor_scan(
                    dbk[:, T - 1::-1], db, EK[:, ::-1], 0.0, ALU.mult, ALU.add), "v_sc")
                B["EK"] = [M["db"]]

            def n1():
                M["n"] = Q.put(DV, [M["nb"], m_nb0], lambda e: e.scalar_tensor_tensor(
                    nf, nbk[:, 1:T + 1], d, nf, ALU.mult, ALU.add), "v_sc")

            def n2():
                M["n"] = Q.put(PL if early else DV, [M["n"], A[n]["euv"]], lambda e: e.tensor_tensor(
                    nf, nf, euv, ALU.add), "p_nd" if early else "v_sc")

            def d1():
                M["d"] = Q.put(DV, [M["db"]], lambda e: e.scalar_tensor_tensor(
                    df, dbk[:, 1:T + 1], d, df, ALU.mult, ALU.add), "v_sc")

            def d2():
                M["d"] = Q.put(PL if early else DV, [M["d"], A[n]["eu"]], lambda e: e.tensor_tensor(
                    df, df, eu, ALU.add), "p_nd" if early else "v_sc")
                B["EU"][set_] = [M["d"], M["n"]]

            def d3():
                if i == 0:
                    M["d"] = Q.put(DV, [M["d"], A[n]["er"]], lambda e: e.scalar_tensor_tensor(
                        df, df, 1e-8, er, ALU.max, ALU.mult), "v_sc")
                    if n in (0, 3) or not early:
                        B["ER"] = [M["d"]]
                else:
                    M["d"] = Q.put(DV, [M["d"]], lambda e: e.tensor_scalar(df, df, 1e-8, None, ALU.max), "v_sc")

            def rc(j):
                M["r"] = Q.put(DV, [M["d"]], lambda e: e.reciprocal(
                    dbk[:, 128 * j:128 * j + 128], df[:, 128 * j:128 * j + 128]), "v_sc")
                if j == 0 and i == 0 and after is not None and n > 2:
                    er_load(after)

            def out():
                M["o"] = Q.put(DV, [M["r"], M["n"]] + B["OY"], lambda e: e.scalar_tensor_tensor(
                    OY[:, :], nf, tf[:, 2, b:b + 1], dbk[:, 0:T], ALU.mult, ALU.mult), "v_sc")
                B["N"][set_] = [M["o"]]

            def store():
                m = M["o"]
                if i == 0:
                    s = b % 2
                    free = y_free.get(b, [])
                    h = Q.put(AC, [m] + free, lambda e: e.activation(yh[s][:, c, :], OY[:, :], ACT.Copy), "a_yh")
                    l = Q.put(PL, [h, m] + free, lambda e: e.tensor_tensor(
                        yl[s][:, c, :], OY[:, :], yh[s][:, c, :], ALU.subtract), "p_yl")
                    y_ready.setdefault(b, []).extend([h, l])
                    B["OY"] = [l, h]
                else:
                    s = Q.dma([m], ratio_s[b, c], OY[:, :], "d_rs")
                    m_ratio[b, c] = s
                    B["OY"] = [s]

            N = n + 1
            head = [(600, s1), (600, s2), (600, s3), (600, s4), (335, lambda: a_min(N)), (660, n1), (600, n2),
                    (0, lambda: a_exp(N)), (660, d1), (600, d2)]
            feed = [(335, lambda: b_min(N)), (0, lambda: a_mul(N)), (0, lambda: b_exp(N)), (0, lambda: b_mul(N))]
            tail = [(500, d3), (880, lambda: rc(0)), (880, lambda: rc(1)), (880, lambda: rc(2)), (880, lambda: rc(3)),
                    (700, out), (0, store)]
            if early:
                head = [head[i] for i in (0, 1, 2, 3, 4, 5, 7, 8)] + [feed[1], head[6], head[9]]
                return head, [feed[0]] + feed[2:], tail
            return (head[:4] + [(0, lambda: e_exp(n))] + head[4:] + feed[:2] + tail[:1] + feed[2:3] + tail[1:3]
                    + feed[3:] + tail[3:])

        def had_steps():
            M = {}

            def first():
                bar = [Q.last[DV, "v_sc"], Q.last[PL, "p_ekv"], Q.last[PL, "p_euv"], Q.last[AC, "a_eu"],
                       Q.last[AC, "a_ek"], Q.last[AC, "a_yh"], Q.last[AC, "a_er"], Q.last[SP, "d_rs"],
                       Q.last[PL, "p_yl"]]
                M["ha"] = bar
                M["out"] = bar
                M["hb"] = bar
                d = Q.dma(bar, hadf[:, :], had_d, "d_had")
                M["hadf"] = d
                M["load"] = Q.dma(bar, HA[:, :], w2_d[0].rearrange("p a d -> p (a d)"), "d_h")

            def level(lv):
                w = 64 << lv
                a = [HA, HB][lv % 2][:, :].rearrange("p (x t w) -> p x t w", t=2, w=w)
                o = [HB, HA][lv % 2][:, :].rearrange("p (x t w) -> p x t w", t=2, w=w)
                waits = [M["load"]] if lv == 0 else [M["lv"]]
                if lv == 0:
                    waits = waits + M["hb"]
                Q.put(DV, waits, lambda e: e.tensor_tensor(
                    o[:, :, 0, :], a[:, :, 0, :], a[:, :, 1, :], ALU.add), "v_h")
                M["lv"] = Q.put(DV, [], lambda e: e.tensor_tensor(
                    o[:, :, 1, :], a[:, :, 0, :], a[:, :, 1, :], ALU.subtract), "v_h")

            def parts(n):
                if n == 0:
                    M["had"] = Q.put(AC, [M["hadf"]], lambda e: e.activation(had[:, :], hadf[:, :], ACT.Copy), "a_had")
                M["hi"] = Q.put(AC, [M["lv"]] + M.get("pe", M["ha"]), lambda e: e.activation(HH[:, :], HA[:, :], ACT.Copy), "a_h")

            def low():
                M["lo"] = Q.put(DV, [M["hi"]] + M.get("pe", M["ha"]), lambda e: e.tensor_tensor(
                    HL[:, :], HA[:, :], HH[:, :], ALU.subtract), "v_h")
                M["hb"] = [M["lo"]]

            def load(n):
                M["load"] = Q.dma_by_scalar([M["lo"], M["hi"]], HA[:, :], w2_d[n + 1].rearrange("p a d -> p (a d)"), "d_h")

            def mult(n, j):
                bank = next_g()
                bk = banks[bank]
                cut = slice(512 * j, 512 * j + 512)
                Q.put(PE, bank_free[bank] + [M["had"], M["hi"], M["lo"]], lambda e: e.matmul(
                    bk[:, :], had[:, :], HH[:, cut], start=True, stop=False))
                m = Q.put(PE, [], lambda e: e.matmul(
                    bk[:, :], had[:, :], HL[:, cut], start=False, stop=True), "pe_h")
                M["pe"] = [m]
                o = Q.put(AC, [m] + M["out"], lambda e: e.activation(
                    HO[:, cut], bk[:, :], ACT.Copy, scale=RSQ), "a_ho")
                bank_free[bank] = [o]
                M["ho"] = o

            def save(n):
                M["out"] = [Q.dma([M["ho"]], w2_s[n].rearrange("p a d -> p (a d)"), HO[:, :], "d_ho")]
                if n == 7:
                    m_w2s[:] = M["out"]

            steps = [(1000, first), (1000, wait), (1000, wait), (1000, wait)]
            for n in range(8):
                steps += [(1250, lambda lv=lv: level(lv)) for lv in range(4)]
                steps += [(1000, lambda n=n: parts(n)), (1000, wait), (1250, low), (1000, wait)]
                if n < 7:
                    steps += [(0, lambda n=n: load(n))]
                steps += [(0, None), (1000, lambda n=n: mult(n, 0)), (0, None), (1000, lambda n=n: mult(n, 1)),
                          (1000, wait), (0, lambda n=n: save(n))]
            return steps

        def wait():
            return

        gi = [0]

        def next_g():
            gi[0] += 1
            return f"G{gi[0] % 2}"

        background = []
        for n in range(4, len(tiles)):
            background += [(cost, fn, n) for cost, fn in scan_steps(n)]
        background += [(cost, fn, len(tiles)) for cost, fn in had_steps()]
        at = [0]
        whole = [False]

        def work(ns):
            while ns > 0 and at[0] < len(background):
                cost, fn, tile = background[at[0]]
                if tile < len(tiles) and tiles[tile][0] == 0 and tiles[tile][1] not in y_free:
                    return
                if tile > len(tiles) and tile - len(tiles) + 3 not in y_free:
                    return
                if fn is None and not whole[0]:
                    return
                at[0] += 1
                if fn is not None:
                    fn()
                ns -= cost

        def work_until(tile):
            while at[0] < len(background) and background[at[0]][2] <= tile:
                fn = background[at[0]][1]
                at[0] += 1
                if fn is not None:
                    fn()

        D = {}
        behind, before = [], []

        def kq(n, which, j, part):
            g, b = order[n]
            wi = windex[which, n]
            slot, ys = W["slot"][wi], b % 2
            if part == 0:
                D["bank"] = next_g()
            bank = D["bank"]
            terms = [((wh[slot][:, 256 * c + 128 * j:256 * c + 128 * j + 128],
                       wl[slot][:, 256 * c + 128 * j:256 * c + 128 * j + 128]),
                      (yh[ys][:, c, :], yl[ys][:, c, :])) for c in range(NC)]
            assert len(y_ready[b]) == 2 * NC
            m = passes(bank, banks[bank][:, :], terms, W["ready"][wi] + y_ready[b], "pe_g", part=(part, 2))
            if part == 1:
                kq_done(n, which, j, bank, m)

        def kq_done(n, which, j, bank, m):
            g, b = order[n]
            wi = windex[which, n]
            slot = W["slot"][wi]
            if j == 1:
                W["free"].append((slot, [m]))
                if g == NG - 1 and which == "q":
                    y_free[b + 2] = [m]
            dst, sig = (qT, sq) if which == "q" else (kT, sk)
            a = Q.put(AC, [m] + D.get("scores", []), lambda e: e.activation(dst[:, j, :], banks[bank][:, :], ACT.Copy), "a_qk")
            bank_free[bank] = [a]
            D[which, j] = a
            etmp = etmps[j]
            p = Q.put(AC, [m] + D.get(("etmp", j), []), lambda e: e.activation(
                etmp[:, :], banks[bank][:, :], ACT.Relu, scale=-1.0), "a_mn")
            bank_free[bank] = [p]
            x2 = Q.put(AC, [p], lambda e: e.activation(etmp[:, :], etmp[:, :], ACT.Exp, scale=-1.0), "a_e")

            def sigma():
                old = D.get("am3" if which == "q" else "dk2", [])
                s = Q.put(DV, [x2, a] + old, lambda e: e.scalar_tensor_tensor(
                    sig[:, j, :], dst[:, j, :], 1.0, etmp[:, :], ALU.add, ALU.max), "v_sg")
                D["etmp", j] = [s]
                D["s" + which, j] = s

            behind.append([2 if which == "k" else 1, sigma])

        def vv(n, half, part):
            g, b = order[n]
            wi = windex["v", n]
            slot, ys = W["slot"][wi], b % 2
            if part == 0:
                D["bank"] = next_g()
            bank = D["bank"]
            bk = banks[bank]
            t = 2 * half + part
            terms = [((yh[ys][:, c, 128 * t:128 * t + 128], yl[ys][:, c, 128 * t:128 * t + 128]),
                      (wh[slot][:, 256 * c:256 * c + 256], wl[slot][:, 256 * c:256 * c + 256])) for c in range(NC)]
            m = passes(bank, bk[:, 256 * part:256 * part + 256], terms, W["ready"][wi] + y_ready[b], "pe_g", free=(part == 0))
            if part == 1:
                vv_done(n, half, bank, m)

        def vv_done(n, half, bank, m, eng=AC):
            wi = windex["v", n]
            slot = W["slot"][wi]
            bk = banks[bank]
            if half == 1:
                W["free"].append((slot, [m]))
            vt = v[n % 2]
            dst, raw = vt[:, 2 * half:2 * half + 2, :, 0:P], bk[:, :].rearrange("p (t h d) -> p t h d", t=2, h=2)
            if eng == AC:
                a = Q.put(AC, [m] + D.get(("u2", n - 2), []), lambda e: e.activation(dst, raw, ACT.Copy), "a_v")
            else:
                a = Q.put(DV, [m], lambda e: e.tensor_copy(dst, raw), "v_v")
            bank_free[bank] = [a]
            D["v", n, half] = a

        def v_scaled(n):
            vt = v[n % 2]
            for j in range(2):
                m = Q.put(PL, [D["v", n, 0], D["v", n, 1], D["omb"]] + D.get("pv", []), lambda e, j=j: e.tensor_tensor(
                    vs[:, :, j, :], vt[:, :, j, 0:P],
                    omb[:, 128 * j:128 * j + 128].rearrange("p (a d) -> p a d", a=1).to_broadcast([P, NSEG, P]),
                    ALU.mult), "p_vs")
            D["vs"] = m

        def load_omb(n):
            g = order[n][0]
            w = [D["vs"]] if "vs" in D else []
            D["omb"] = Q.dma_by_scalar(w + [m_beta[1]], omb[:, :],
                             beta_s[1, 2 * g:2 * g + 2, :].rearrange("(o h) d -> o (h d)", o=1).to_broadcast([P, 256]), "d_om")

        def load_bet(n):
            g = order[n][0]
            w = D.get("t2_3", [])
            D["bet"] = Q.dma_by_scalar(w + [m_beta[0]], bet[:, :],
                             beta_s[0, 2 * g:2 * g + 2, :].rearrange("(o h) d -> o (h d)", o=1).to_broadcast([P, 256]), "d_be")

        def wo(n, i):
            wi = windex["o", (n, i)]
            slot = W["slot"][wi]
            if i == 0:
                D["wo_banks"] = [next_g(), next_g()]
            for dc in range(NC):
                bank = D["wo_banks"][dc // 2]
                out = banks[bank][:, 256 * (dc % 2):256 * (dc % 2) + 256]
                pairs = []
                for jj in range(2):
                    lo = 512 * jj + 128 * dc
                    j = 2 * i + jj
                    pairs += [(wh[slot][:, lo:lo + 128], ah[:, j, :]), (wh[slot][:, lo:lo + 128], al[:, j, :]),
                              (wl[slot][:, lo:lo + 128], ah[:, j, :])]
                for k, (a, c) in enumerate(pairs):
                    start = i == 0 and k == 0 and dc % 2 == 0
                    stop = i == 7 and k == 5
                    w = (W["ready"][wi] + D["att"] + bank_free[bank]) if k == 0 else []
                    m = Q.put(PE, w, lambda e, a=a, c=c, out=out, start=start, stop=stop: e.matmul(
                        out, a, c, start=start, stop=stop, skip_group_check=True), "pe_o" if k == 5 else None)
                if i == 7 and dc % 2 == 1:
                    D["wo_done", dc // 2] = m
            W["free"].append((slot, [m]))
            if i < 7:
                return
            D["wo"] = [m]
            b, half = order[n][1], (n % 8) // 4
            for dc in range(NC):
                bank = D["wo_banks"][dc // 2]
                src_ = banks[bank][:, 256 * (dc % 2):256 * (dc % 2) + 256].rearrange("p (h s r) -> p h s r", h=8, s=4)
                dst = xb[:, dc, :].rearrange("p (s h r) -> p h s r", s=4, h=16)[:, 8 * half:8 * half + 8]
                a = Q.put(DV, [D["wo_done", dc // 2], m_xb[b]], lambda e, src_=src_, dst=dst: e.tensor_tensor(
                    dst, dst, src_, ALU.add), "v_x")
                bank_free[bank] = [a]
            if half == 1:
                def keep(dc):
                    m_x1[b] = Q.dma_by_scalar([a], x1_s[b, :, dc, :], xb[:, dc, :], "d_x1")

                def fetch(dc):
                    m_xb[b + 1] = Q.dma([m_x1[b]], xb[:, dc, :], xT_d[b + 1, :, dc, :], "d_xb")

                later.extend(lambda dc=dc: keep(dc) for dc in range(NC))
                if b + 1 < NB:
                    later.extend(lambda dc=dc: fetch(dc) for dc in range(NC))
                else:
                    while later:
                        later.pop(0)()

        m_x1 = {}
        later = []

        def seg(s):
            return slice(SEG * s, SEG * s + SEG)

        def s1(n):
            for j in range(2):
                bk = banks[f"Y{j}"]
                for s in range(3):
                    m = Q.put(PE, ([D["sk", j], m_id] + bank_free[f"Y{j}"]) if s == 0 else [], lambda e, j=j, s=s, bk=bk: e.transpose(
                        bk[:, seg(s)], sk[:, j, seg(s)], ident[:, :]), "pe_kt" if s == 2 else None)
                a = Q.put(AC, [m] + D.get(("u2", n - 1), []), lambda e, j=j, bk=bk: e.activation(
                    kn[:, j, :, :], bk[:, 0:384].rearrange("p (s k) -> p s k", s=3), ACT.Copy), "a_kn")
                D["kn", j] = a
                bank_free[f"Y{j}"] = [a]
            for j in range(2):
                bk = banks[f"X{j}"]
                for s in range(NSEG):
                    m = Q.put(PE, ([D["q", j], D["k", j]] + bank_free[f"X{j}"]) if s == 0 else [], lambda e, j=j, s=s, bk=bk: e.matmul(
                        bk[:, seg(s)], qT[:, j, seg(s)], kT[:, j, seg(s)], start=True, stop=True), "pe_s" if s == 3 else None)
                D["scores"] = [m]
                for s in range(NSEG):
                    w = [m, m_mk] + D.get("at", []) + list(m_beta[0:2])
                    t = Q.put(DV, w if s == 0 else [], lambda e, j=j, s=s, bk=bk: e.tensor_tensor_reduce(
                        S[:, j, seg(s)], bk[:, seg(s)], mask[:, :], 1.0, NEG, ALU.add, ALU.max,
                        st[:, 0, j, s:s + 1]), "v_mx")
                bank_free[f"X{j}"] = [t]
                t = Q.put(DV, [t] + D.get(("exp", j), []), lambda e, j=j: e.tensor_scalar(
                    st[:, 1, j, :], st[:, 0, j, :], -SCALE, None, ALU.mult), "v_mx")
                for s in range(NSEG):
                    a = Q.put(AC, [t] + D.get("rd", []), lambda e, j=j, s=s: e.activation(
                        S[:, j, seg(s)], S[:, j, seg(s)], ACT.Exp, bias=st[:, 1, j, s:s + 1], scale=SCALE,
                        accum_out=st[:, 2, j, s:s + 1]), "a_p")
                D["exp", j] = [a]

        def update(n, s):
            for j in range(2):
                bk = banks[f"Z{j}"]
                rhs = v[n % 2][:, 0, j, :] if s == 0 else delta[:, j, :]
                w = [D["kn", j], m_beta[2]] + ([D["v", n, 0]] if s == 0 else [D["delta", j]])
                m = Q.put(PE, w + bank_free[f"Z{j}"], lambda e, j=j, bk=bk, rhs=rhs: e.matmul(
                    bk[:, 258:387], kn[:, j, s, :], rhs, start=True, stop=True), "pe_u")
                prev = mem0[:, :] if s == 0 else mem[:, j, :]
                t = Q.put(DV, [m] + D.get("am", []) + D.get(("mem", j), []), lambda e, j=j, bk=bk, prev=prev: e.tensor_tensor(
                    mem[:, j, :], bk[:, 258:387], prev, ALU.add), "v_mem")
                bank_free[f"Z{j}"] = [t]
                D["mem", j] = [t]
            if s == 2:
                D["u2", n] = [m]

        def recall(n, s):
            for j in range(2):
                bk = banks[f"Z{j}"]
                w = bank_free[f"Z{j}"] + D["mem", j] + [D["sq", j]]
                if s < 3:
                    Q.put(PE, w, lambda e, j=j, bk=bk: e.matmul(
                        bk[:, 0:129], sk[:, j, seg(s)], mem[:, j, :], start=True, stop=True))
                m = Q.put(PE, w, lambda e, j=j, bk=bk: e.matmul(
                    bk[:, 129:258], sq[:, j, seg(s)], mem[:, j, :], start=True, stop=True), "pe_am")
                lo = 0 if s < 3 else 1
                t = Q.put(DV, [m] + D.get(("rz", j), []), lambda e, j=j, bk=bk, lo=lo: e.reciprocal(
                    rz[:, j, lo:2], bk[:, 128 + 129 * lo:258:129]), "v_r")
                r = t
                if s < 3:
                    t = Q.put(DV, [r, D["v", n, 0], D["v", n, 1]], lambda e, j=j, bk=bk: e.scalar_tensor_tensor(
                        delta[:, j, 0:P], bk[:, 0:128], rz[:, j, 0:1], v[n % 2][:, s, j, 0:P], ALU.mult, ALU.subtract,
                        reverse1=True), "v_r")
                    D["delta", j] = t
                t = Q.put(DV, [r, D["bet"]], lambda e, j=j, bk=bk: e.scalar_tensor_tensor(
                    t2[:, j, s - 1, :], bk[:, 129:257], rz[:, j, 1:2], bet[:, 128 * j:128 * j + 128],
                    ALU.mult, ALU.mult), "v_r")
                bank_free[f"Z{j}"] = [t]
                D["rz", j] = [t]
                D["t2", j, s] = t
            D["am"] = [m]
            if s == 3:
                D["am3"] = [m]
                D["t2_3"] = [t]
            if s == 2:
                D["dk2"] = [m]

        def turn_p(n):
            for j in range(2):
                bk = banks[f"Y{j}"]
                for s in range(NSEG):
                    m = Q.put(PE, (D["exp", j] + [m_id] + bank_free[f"Y{j}"]) if s == 0 else [], lambda e, j=j, s=s, bk=bk: e.transpose(
                        bk[:, seg(s)], S[:, j, seg(s)], ident[:, :]), "pe_pt" if s == 3 else None)
                a = Q.put(AC, [m] + D.get("pv", []), lambda e, j=j, bk=bk: e.activation(
                    pT[:, j, :], bk[:, :], ACT.Copy), "a_pt")
                D["pT", j] = a
                D["p_read", j] = m
                bank_free[f"Y{j}"] = [a]
            D["rd"] = [Q.put(DV, D["exp", 1] + D["exp", 0], lambda e: e.reciprocal(
                st[:, 3, :, :], st[:, 2, :, :]), "v_rd")]

        def pv(n):
            for j in range(2):
                bk = banks[f"X{j}"]
                for s in range(NSEG):
                    m = Q.put(PE, ([D["pT", j], D["vs"]] + bank_free[f"X{j}"]) if s == 0 else [], lambda e, j=j, s=s, bk=bk: e.matmul(
                        bk[:, seg(s)], pT[:, j, seg(s)], vs[:, s, j, :], start=True, stop=True), "pe_pv" if s == 3 else None)
                D["ad", j] = m
            D["pv"] = [m]

        def join(n, s):
            for j in range(2):
                bk = banks[f"X{j}"]
                w = [D["ad", j], D["p_read", j]] + D["rd"]
                if s == 0:
                    t = Q.put(DV, w, lambda e, j=j, bk=bk: e.tensor_scalar(
                        S[:, j, seg(0)], bk[:, seg(0)], st[:, 3, j, 0:1], None, ALU.mult), "v_at")
                else:
                    t = Q.put(DV, w + [D["t2", j, s]], lambda e, j=j, bk=bk: e.scalar_tensor_tensor(
                        S[:, j, seg(s)], bk[:, seg(s)], st[:, 3, j, s:s + 1], t2[:, j, s - 1, :],
                        ALU.mult, ALU.add), "v_at")
                bank_free[f"X{j}"] = [t]
                D["join", j] = t

        def turn_att(n):
            if n % 4 == 0:
                D["att"] = []
            for j in range(2):
                bk = banks[f"Y{j}"]
                for s in range(NSEG):
                    m = Q.put(PE, ([D["join", j]] + bank_free[f"Y{j}"]) if s == 0 else [], lambda e, j=j, s=s, bk=bk: e.transpose(
                        bk[:, seg(s)], S[:, j, seg(s)], ident[:, :]), "pe_at" if s == 3 else None)
                D["at"] = [m]
                h = 2 * (n % 4) + j
                turned = bk[:, :].rearrange("p (s j) -> p j s", j=16)
                hi, lo = ah[:, :, 32 * h:32 * h + 32], al[:, :, 32 * h:32 * h + 32]
                a = Q.put(AC, [m] + D.get("wo", []), lambda e, hi=hi, turned=turned: e.activation(hi, turned, ACT.Copy), "a_at")

                def low(j=j, a=a, hi=hi, lo=lo, turned=turned):
                    t = Q.put(DV, [a], lambda e: e.tensor_tensor(lo, turned, hi, ALU.subtract), "v_al")
                    bank_free[f"Y{j}"] = [t]
                    D["att"] = D["att"] + [a, t]

                before.append(low)

        z_ready = {}
        F = {}
        rt_free, sg_free = {}, {}

        def modulate(b, bar=None):
            z_ready[b] = []
            M = {}

            def load():
                if not rt_free:
                    w = [Q.last[DV, "v_h"], Q.last[AC, "a_ho"], Q.last[PE, "pe_h"],
                         Q.last[AC, "a_h"], Q.last[SP, "d_ho"]]
                    rt_free.update({i: w for i in range(2)})
                    sg_free.update({i: w for i in range(6)})
                for c in range(NC):
                    M["sg", c] = Q.dma(sg_free[c] + [m_x1[b]], sg[c][:, :], x1_s[b, :, c, :], f"d_sg{c}")
                for c in range(2):
                    ratio(c)

            def ratio(c):
                s = c % 2
                M["rt", c] = Q.dma(rt_free[s] + [m_ratio[b, c]], rt[s][:, :], ratio_s[b, c], f"d_rt{s}")

            def sigmoid():
                for c in range(NC):
                    M["a", c] = Q.put(AC, [M["sg", c]], lambda e, c=c: e.activation(
                        sg[c][:, :], sg[c][:, :], ACT.Sigmoid), "a_z")

            def times(c):
                s = c % 2
                M["t", c] = Q.put(DV, [M["a", c], M["rt", c]], lambda e: e.tensor_tensor(
                    sg[c][:, :], sg[c][:, :], rt[s][:, :], ALU.mult), "v_z")
                rt_free[s] = [M["t", c]]
                if c < 2:
                    ratio(c + 2)

            def parts(c):
                w = y_free[4 + b] if bar is None else bar
                h = Q.put(AC, [M["t", c]] + w, lambda e: e.activation(zh[b][:, c, :], sg[c][:, :], ACT.Copy), "a_z")
                l = Q.put(PL if bar is None else DV, [M["t", c], h] + w, lambda e: e.tensor_tensor(
                    zl[b][:, c, :], sg[c][:, :], zh[b][:, c, :], ALU.subtract), "p_z" if bar is None else "v_zl")
                sg_free[c] = [l, h]
                z_ready[b] += [h, l]

            return ([(1500, load), (1500, wait), (1500, wait), (1500, sigmoid), (1500, wait)]
                    + [(1000, lambda c=c: times(c)) for c in range(NC)],
                    [(800, lambda c=c: parts(c)) for c in range(NC)])

        background += [(cost, fn, len(tiles) + 1) for part in modulate(0) for cost, fn in part]
        background += [(cost, fn, len(tiles) + 2) for part in modulate(1) for cost, fn in part]

        ffn = [(g, b) for g in range(NG) for b in range(NB)]
        bar = []
        names = list(banks)
        bi = [0]

        def next_bank():
            bi[0] += 1
            return names[bi[0] % 8]

        sgi = [0]
        h_used = {0: [], 1: bar}
        U = {}

        def up_part(n, bank_of, j, k):
            g, b = ffn[n]
            last = n + 1 == len(ffn) or ffn[n + 1][0] != g
            wi = windex[k, g]
            slot = W["slot"][wi]
            U["bank", k] = bank_of()
            bk = banks[U["bank", k]]
            assert len(z_ready[b]) == 2 * NC
            terms = [((wh[slot][:, 256 * c + 128 * j:256 * c + 128 * j + 128],
                       wl[slot][:, 256 * c + 128 * j:256 * c + 128 * j + 128]),
                      (zh[b][:, c, :], zl[b][:, c, :])) for c in range(NC)]
            U[k] = passes(U["bank", k], bk[:, :], terms, W["ready"][wi] + z_ready[b], "pe_g")
            if last and j == 1:
                W["free"].append((slot, [U[k]]))
            if k == "1":
                U["s"] = s = 4 + sgi[0] % 2 if n < 2 else sgi[0] % 6
                sgi[0] += 1
                t_ = sg[s]
                a = Q.put(AC, [U["1"]] + sg_free[s], lambda e: e.activation(t_[:, :], bk[:, :], ACT.Sigmoid), "a_f")
                U["t"] = Q.put(DV, [a], lambda e: e.tensor_tensor(t_[:, :], bk[:, :], t_[:, :], ALU.mult), "v_f")
                bank_free[U["bank", "1"]] = [U["t"]]
                return
            s = U["s"]
            t_ = sg[s]
            t = Q.put(DV, [U["t"], U["3"]], lambda e: e.tensor_tensor(t_[:, :], bk[:, :], t_[:, :], ALU.mult), "v_f")
            bank_free[U["bank", "3"]] = [t]
            o = n % 2
            h = Q.put(AC, [t] + h_used[o], lambda e: e.activation(hh[o][:, j, :], t_[:, :], ACT.Copy), "a_f")
            l = Q.put(PL, [h, t] + h_used[o], lambda e: e.tensor_tensor(
                hl[o][:, j, :], t_[:, :], hh[o][:, j, :], ALU.subtract), "p_f")
            sg_free[s] = [l, h]
            F.setdefault(n, []).extend([h, l])

        def up(n):
            for j in range(2):
                for k in "13":
                    up_part(n, next_bank, j, k)
                split_weights(1)

        def now(steps):
            for fn in steps:
                fn()

        def early_constants():
            c = Q.put(DV, [e_b], lambda e: e.tensor_scalar_add(bt, bt, 1.0), "v_c")
            c = Q.put(DV, [c], lambda e: e.reciprocal(S[0:H, 1, P:2 * P], bt), "v_c")
            c = Q.put(DV, [c], lambda e: e.tensor_scalar(
                S[0:H, 1, 2 * P:3 * P], S[0:H, 1, P:2 * P], -1.0, 1.0, ALU.mult, ALU.add), "v_c")
            a = Q.dma([c], beta_s[0], S[0:H, 1, P:2 * P], "d_b0")
            b = Q.dma([c], beta_s[1], S[0:H, 1, 2 * P:3 * P], "d_b1")
            for t in v:
                Q.put(DV, [], lambda e, t=t: e.memset(t[:, :, :, P:P + 1], 1.0), "v_c")
            Q.put(DV, [], lambda e: e.memset(mem0[:, 0:P], 0.0), "v_c")
            Q.put(DV, [], lambda e: e.memset(mem0[:, P:P + 1], 1.0 / P), "v_c")
            d = Q.put(DV, [], lambda e: e.memset(delta[:, :, P:P + 1], 1.0), "v_c")
            return a, b, d

        e_w = Q.put(AC, [m_wu], lambda e: e.activation(dec0[:, :, :], wu[:, 0:4:2, :], ACT.Exp), "a_c")
        e_w = Q.put(AC, [e_w], lambda e: e.activation(dec0[:, :, :], dec0[:, :, :], ACT.Exp, scale=-1.0), "a_c")
        c1 = Q.put(DV, [m_cb], lambda e: e.tensor_reduce(
            tf[:, 0, :], cb.rearrange("p (b t) -> p b t", b=NB), AX_X, ALU.add), "v_c")
        e_t = Q.put(AC, [c1], lambda e: e.activation(tf[:, 1, :], tf[:, 0, :], ACT.Exp, scale=-1.0), "a_c")
        a_min(0)
        c1 = Q.put(DV, [e_t], lambda e: e.tensor_scalar_add(tf[:, 1, :], tf[:, 1, :], 1.0), "v_c")
        c1 = Q.put(DV, [c1], lambda e: e.reciprocal(tf[:, 0, :], tf[:, 1, :]), "v_c")
        c1 = Q.put(DV, [c1], lambda e: e.tensor_scalar(tf[:, 1, :], tf[:, 0, :], 0.5, 0.5, ALU.mult, ALU.add), "v_c")
        m_s = Q.put(DV, [c1], lambda e: e.tensor_scalar(tf[:, 2, :], tf[:, 0, :], 0.2, 0.8, ALU.mult, ALU.add), "v_c")
        for b in range(NB):
            m_dec = Q.put(DV, [c1, m_s, e_w], lambda e, b=b: e.tensor_scalar(
                dec[:, b, :, :], dec0[:, :, :], tf[:, 1, b:b + 1], None, ALU.mult), "v_c")
        m_cut = Q.put(DV, [m_wu], lambda e: e.tensor_scalar(
            ucut[:, :, :], wu[:, 1:4:2, :], -1.0, 30.0, ALU.mult, ALU.add), "v_c")
        b_min(0)
        for t in (NBK, DBK, nbk1, dbk1):
            m_nb0 = Q.put(DV, [], lambda e, t=t: e.memset(t[:, T:T + 1], 0.0), "v_c")

        a_exp(0)
        a_mul(0)
        b_exp(0)
        b_mul(0)
        e_b = Q.put(AC, [m_bt], lambda e: e.activation(bt, bt, ACT.Exp, scale=-1.0), "a_c")
        e_exp(0)
        load_halves()
        m_xb = {0: Q.dma([], xb[:, :, :], xT_d[0], "d_xb")}
        m_id = Q.dma([], ident[:, :], ident_d, "d_id")
        m_mk = Q.dma([], mask[:, :], mask_d, "d_mk")

        startup = [scan_steps(n) for n in range(4)]
        at_ = {"v0": "G0", "v1": "G1", "k0": "X0", "k1": "X1", "q0": "Y0", "q1": "Y1"}
        done = {}

        def chunk(c):
            for what, bank in at_.items():
                kind, i = what[0], int(what[1])
                if windex[kind, 0] not in W["ready"]:
                    split_weights(1)
                wi = windex[kind, 0]
                slot = W["slot"][wi]
                hi, lo = wh[slot], wl[slot]
                if kind == "v":
                    jobs = [(banks[bank][:, 256 * p:256 * p + 256],
                             yh[0][:, c, 256 * i + 128 * p:256 * i + 128 * p + 128],
                             yl[0][:, c, 256 * i + 128 * p:256 * i + 128 * p + 128],
                             hi[:, 256 * c:256 * c + 256], lo[:, 256 * c:256 * c + 256]) for p in range(2)]
                else:
                    cols = slice(256 * c + 128 * i, 256 * c + 128 * i + 128)
                    jobs = [(banks[bank][:, :], hi[:, cols], lo[:, cols], yh[0][:, c, :], yl[0][:, c, :])]
                for p, (out, lh, ll, rh, rl) in enumerate(jobs):
                    for k, (a, d) in enumerate(((lh, rh), (lh, rl), (ll, rh))):
                        start = c == 0 and p == 0 and k == 0
                        last = c == NC - 1 and p == len(jobs) - 1 and k == 2
                        w = W["ready"][wi] + y_ready[0][2 * c:2 * c + 2] if k == 0 and p == 0 else []
                        m = Q.put(PE, w, lambda e, out=out, a=a, d=d, start=start, c=c, k=k: e.matmul(
                            out, a, d, start=start, stop=(c == NC - 1 and k == 2), skip_group_check=True),
                            "pe_g" if last else None)
                done[what] = m

        def seq(steps):
            now(fn for _, fn in steps)

        seq(startup[0][0] + startup[0][1])
        e_exp(1)
        seq(startup[1][0] + startup[1][1])
        split_weights(1)
        seq(startup[0][2])
        split_weights(1)
        e_exp(2)
        seq(startup[2][0] + startup[2][1])
        split_weights(1)
        chunk(0)
        m_beta = early_constants()
        seq(startup[1][2])
        chunk(1)
        e_exp(3)
        seq(startup[3][0] + startup[3][1])
        seq(startup[2][2])
        chunk(2)
        seq(startup[3][2])
        chunk(3)
        load_omb(0)
        load_bet(0)
        for j in range(2):
            kq_done(0, "k", j, f"X{j}", done[f"k{j}"])
            vv_done(0, j, f"G{j}", done[f"v{j}"], DV)
            behind.pop(0)[1]()
        for j in range(2):
            kq_done(0, "q", j, f"Y{j}", done[f"q{j}"])
            behind.pop(0)[1]()
        v_scaled(0)
        split_weights(2)

        def ripe():
            for item in behind:
                item[0] -= 1
            due = [fn for age, fn in behind if age == 0]
            behind[:] = [item for item in behind if item[0] > 0]
            return due

        ups = {"k00": (0, "1"), "k10": (0, "3"), "q00": (1, "1"), "q10": (1, "3")}

        def fill(n, what, ns):
            due = ripe()
            if later:
                later.pop(0)()
            if n < len(order):
                if what[0] == "v":
                    vv(n, int(what[1]), int(what[2]))
                    if what == "v11":
                        D["vs_due"] = n
                else:
                    kq(n, what[0], int(what[1]), int(what[2]))
            elif what in ups:
                work_until(len(tiles) + 1)
                up_part(0, next_g, *ups[what])
            split_weights(1)
            while before:
                before.pop(0)()
            if at[0] == 0 or background[at[0] - 1][2] >= len(tiles):
                ns = max(ns, LATE)
            whole[0] = what[-1] == "1" or n == len(order)
            work(ns)
            whole[0] = False
            now(due)

        for n in range(len(order)):
            nx = n + 1
            if nx < len(order):
                b = order[nx][1]
                if b not in y_ready or len(y_ready[b]) < 2 * NC:
                    work_until([i for i, t in enumerate(tiles) if t == (0, b, NC - 1)][0])
            burst = n % 4 == 0 and n > 0
            pieces = ["v00", "v01", "v10", "v11", "k00", "k01", "k10", "k11", "q00", "q01", "q10", "q11"]
            todo = [0]

            def between(k):
                if burst:
                    if todo[0] < 8:
                        due = ripe()
                        wo(n - 1, todo[0])
                        split_weights(1)
                        work(BURST[todo[0]])
                        todo[0] += 1
                        now(due)
                else:
                    for _ in range(k):
                        fill(nx, pieces[todo[0]], STEADY[todo[0]])
                        todo[0] += 1

            s1(n)
            if n > 0:
                load_bet(n)
            if nx < len(order):
                load_omb(nx)
            between(1)
            update(n, 0)
            between(1)
            recall(n, 1)
            between(2)
            turn_p(n)
            update(n, 1)
            between(1)
            recall(n, 2)
            pv(n)
            join(n, 0)
            if nx < len(order) and not burst:
                v_scaled(nx)
            between(2)
            update(n, 2)
            join(n, 1)
            between(1)
            join(n, 2)
            recall(n, 3)
            join(n, 3)
            between(2)
            if burst:
                while todo[0] < 8:
                    between(1)
            turn_att(n)
            if n == len(order) - 1:
                between(2)
                now(fn for _, fn in behind)
                behind.clear()
            elif burst:
                for p in pieces:
                    fill(nx, p, AFTER)
                    if p == "v11" and nx < len(order):
                        v_scaled(nx)
            else:
                between(2)
            whole[0] = True
            work(END)
            whole[0] = False
        for i in range(8):
            split_weights(1)
            wo(len(order) - 1, i)
            work(3 * END)
            if i == 3:
                work_until(len(tiles) + 2)
                z2 = modulate(2, bar)
                now(fn for _, fn in z2[0])
        apart = ["p_wh", "p_wl", "a_wh"] + [f"d_w{i}" for i in range(NSTAGE)]
        xbar = [m for (eng, name), m in Q.last.items() if name not in apart]
        bar[:] = [m for m in xbar if m[0] != "d_x1"]
        split_weights(3)
        m_x = {}

        def load_x(b):
            m_x[b] = Q.dma(xbar + [m_x1[b]], x[:, b, :, :], x1_s[b], f"d_xx{b}")

        def down(n):
            g, b = ffn[n]
            last = n + 1 == len(ffn) or ffn[n + 1][0] != g
            wi = windex["2", g]
            slot = W["slot"][wi]
            o = n % 2
            for dc in range(NC):
                bank = next_bank()
                terms = [((wh[slot][:, 512 * j + 128 * dc:512 * j + 128 * dc + 128],
                           wl[slot][:, 512 * j + 128 * dc:512 * j + 128 * dc + 128]),
                          (hh[o][:, j, :], hl[o][:, j, :])) for j in range(2)]
                m = passes(bank, banks[bank][:, :], terms, W["ready"][wi] + F[n], "pe_g")
                a = Q.put(DV, [m, m_x[b]], lambda e, bank=bank, dc=dc: e.tensor_tensor(
                    x[:, b, dc, :], x[:, b, dc, :], banks[bank][:, :], ALU.add), "v_x")
                bank_free[bank] = [a]
                if g == NG - 1:
                    outs.append(Q.dma([a], out_d[b, :, dc, :], x[:, b, dc, :], "d_out"))
            h_used[o] = [m]
            if last:
                W["free"].append((slot, [m]))
                split_weights(2)

        outs = []
        for n in range(len(ffn) + 1):
            if 0 < n < len(ffn):
                up(n)
            if n == 1:
                now(fn for _, fn in z2[1])
            if n == 0:
                load_x(0)
            if n > 0:
                down(n - 1)
            if n == 1:
                z3 = modulate(3, bar)
                now(fn for _, fn in z3[0])
                now(fn for _, fn in z3[1])
                for b in (1, 2, 3):
                    load_x(b)
        Q.put(SP, [outs[-1]], None)

        Q.run(ctx.enter_context(nc.Block()))


_OUT = (NB, P, NC, T)


def kernel(x, fside_BxSxS_0, cond_512, L0_cond_w, L0_cond_u, L0_attn_Wq, L0_attn_Wk, L0_attn_Wv, L0_attn_Wo,
           L0_attn_betas, L0_cond2_w, L0_cond2_u, L0_ffn_W1, L0_ffn_W2, L0_ffn_W3):
    import numpy as np
    import concourse.bacc as bacc
    from concourse.bass_utils import run_bass_kernel_spmd as run

    def fresh(a):
        return np.ascontiguousarray(a)

    def channels(a):
        a = np.asarray(a).reshape(NB, T, NC, P)
        return fresh(a.transpose(0, 3, 2, 1))

    def columns(w):
        a = np.asarray(w).reshape(NC, P, NG, 256)
        return fresh(a.transpose(2, 1, 0, 3)).reshape(NG, P, 2, 512)

    ident = np.eye(P, dtype=np.float32)
    mask = np.where(np.tril(np.ones((P, P), bool)), np.float32(0), np.float32(NEG)).astype(np.float32)
    had = np.ones((1, 1), np.float32)
    while had.shape[0] < P:
        had = np.block([[had, had], [had, -had]]).astype(np.float32)
    wo = fresh(np.asarray(L0_attn_Wo).reshape(NG, 2, P, C).transpose(0, 2, 1, 3))
    w2 = np.asarray(L0_ffn_W2).T.reshape(16, P, 8, 64)
    wu = np.stack([np.asarray(a).reshape(NC, P).T for a in (L0_cond_w, L0_cond_u, L0_cond2_w, L0_cond2_u)], 1)
    arrays = {
        "xT": channels(x), "fT": channels(fside_BxSxS_0),
        "cond": fresh(np.asarray(cond_512).reshape(1, NB * P)), "wu": fresh(wu),
        "wq": columns(L0_attn_Wq), "wk": columns(L0_attn_Wk), "wv": columns(L0_attn_Wv),
        "wo": wo, "betas": fresh(np.asarray(L0_attn_betas).reshape(H, P)),
        "w1": columns(np.asarray(L0_ffn_W1).T), "w3": columns(np.asarray(L0_ffn_W3).T),
        "w2": fresh(w2.transpose(2, 1, 0, 3)), "ident": ident, "mask": mask, "had": had,
    }
    nc = bacc.Bacc("TRN2", target_bir_lowering=False, num_devices=1)
    args = [nc.dram_tensor("in_" + k, list(a.shape), F32, kind="ExternalInput").ap() for k, a in arrays.items()]
    args.append(nc.dram_tensor("out_0", list(_OUT), F32, kind="ExternalOutput").ap())
    adaln_attn_ffn(nc, *args)
    r = run(nc, [{"in_" + k: a for k, a in arrays.items()}], core_ids=[0])
    got = np.asarray(r.results[0]["out_0"])
    return np.ascontiguousarray(got.transpose(0, 3, 2, 1)).reshape(NB, T, C)
```
